# Optimizing a Trainium2 kernel written in Bass

```python
import numpy as np
import jax
import jax.numpy as jnp

def _softmax(x, axis=-1):
    return jax.nn.softmax(x, axis=axis)

def _gelu(x):
    return jax.nn.gelu(x, approximate=True)

def _silu(x):
    return jax.nn.silu(x)

def _sigmoid(x):
    return jax.nn.sigmoid(x)

def _layernorm(x, axis=-1, eps=1e-05):
    m = jnp.mean(x, axis=axis, keepdims=True)
    v = jnp.var(x, axis=axis, keepdims=True)
    return (x - m) / jnp.sqrt(v + eps)

def _scatter_add(tgt, idx, src, axis=0):
    return tgt.at[idx].add(src)

def _segment_sum(src, seg, n):
    return jax.ops.segment_sum(src, seg, n)
kernel_name = 'mk_prb_d1_jaxref_r4_0bb327'

def setup_inputs(seed: int=0):
    np.random.seed(seed)
    _w = jnp.asarray

    def _L0_attn_setup():
        import jax, jax.numpy as jnp
        import numpy as np
        H = 16
        SEG = 512
        DIL = 8
        BLOCK_M = 64
        key = jax.random.key(seed)
        k1, k2, k3 = jax.random.split(key, 3)
        B, M, D = (2, 2048, 256)
        x = jax.random.normal(k1, (B, M, D), dtype=jnp.float32)
        Wqkv = jax.random.normal(k2, (3 * D, D), dtype=jnp.float32) * 0.02
        Wout = jax.random.normal(k3, (D, D), dtype=jnp.float32) * 0.02
        return {'x': x, 'Wqkv': Wqkv, 'Wout': Wout}
    _L0_attn_in = _L0_attn_setup()

    def _L0_ffn_setup():
        import jax, jax.numpy as jnp
        import numpy as np
        HIDDEN = 256
        INTER = 1024
        key = jax.random.key(seed)
        k1, k2, k3, k4, k5 = jax.random.split(key, 5)
        hidden_states = jax.random.normal(k1, (4, 512, HIDDEN), dtype=jnp.float32)
        W1 = jax.random.normal(k2, (HIDDEN, INTER), dtype=jnp.float32) * (1.0 / np.sqrt(HIDDEN))
        b1 = jax.random.normal(k3, (INTER,), dtype=jnp.float32) * 0.02
        W2 = jax.random.normal(k4, (INTER, HIDDEN), dtype=jnp.float32) * (1.0 / np.sqrt(INTER))
        b2 = jax.random.normal(k5, (HIDDEN,), dtype=jnp.float32) * 0.02
        return {'hidden_states': hidden_states, 'W1': W1, 'b1': b1, 'W2': W2, 'b2': b2}
    _L0_ffn_in = _L0_ffn_setup()
    _d = {'L0_attn_x': _L0_attn_in['x'], 'L0_attn_Wqkv': _L0_attn_in['Wqkv'], 'L0_attn_Wout': _L0_attn_in['Wout'], 'L0_ffn_W1': _L0_ffn_in['W1'], 'L0_ffn_b1': _L0_ffn_in['b1'], 'L0_ffn_W2': _L0_ffn_in['W2'], 'L0_ffn_b2': _L0_ffn_in['b2']}
    _x0 = _d['L0_attn_x']
    _d['L0_attn_x'] = jax.random.normal(jax.random.fold_in(jax.random.key(seed), 1), (16, 1024, 256), dtype=_x0.dtype)
    del _x0
    return _d

def reference(L0_attn_x, L0_attn_Wqkv, L0_attn_Wout, L0_ffn_W1, L0_ffn_b1, L0_ffn_W2, L0_ffn_b2):

    def _L0_attn_ref(x, Wqkv, Wout):
        import jax, jax.numpy as jnp
        import numpy as np
        H = 16
        SEG = 512
        DIL = 8
        BLOCK_M = 64
        B, M, D = x.shape
        hd = D // H
        scale = hd ** (-0.5)
        S = M // SEG
        Kn = SEG // DIL
        nb = SEG // BLOCK_M
        qkv = jnp.einsum('bmd,ed->bme', x, Wqkv).reshape(B, M, 3, H, hd)
        qkv = jnp.transpose(qkv, (2, 0, 3, 1, 4))
        q, k, v = (qkv[0] * scale, qkv[1], qkv[2])
        q4 = q.reshape(B, H, S, SEG, hd)
        k4 = k.reshape(B, H, S, SEG, hd)[:, :, :, ::DIL]
        v4 = v.reshape(B, H, S, SEG, hd)[:, :, :, ::DIL]
        scores = jnp.einsum('bhspd,bhskd->bhspk', q4, k4)
        scores = scores.reshape(B, H, S, nb, BLOCK_M, Kn)
        c = jnp.max(scores, axis=4, keepdims=True)
        w = jnp.exp(scores - c)
        den = jnp.sum(w, axis=-1) + 1e-10
        num = jnp.einsum('bhsnmk,bhskd->bhsnmd', w, v4)
        out = num / den[..., None]
        out = out.reshape(B, H, M, hd)
        out = jnp.transpose(out, (0, 2, 1, 3)).reshape(B, M, D)
        return jnp.einsum('bmd,ed->bme', out, Wout)

    def _L0_ffn_ref(hidden_states, W1, b1, W2, b2):
        import jax, jax.numpy as jnp
        import numpy as np
        HIDDEN = 256
        INTER = 1024
        h = jax.nn.relu(jnp.einsum('bsh,hi->bsi', hidden_states, W1) + b1)
        return jnp.einsum('bsi,ih->bsh', h, W2) + b2
    x = L0_attn_x
    xn = _layernorm(x, axis=-1)
    x = x + _L0_attn_ref(xn, L0_attn_Wqkv, L0_attn_Wout) + _L0_ffn_ref(xn, L0_ffn_W1, L0_ffn_b1, L0_ffn_W2, L0_ffn_b2)
    return x

_drawn_inputs = setup_inputs


def setup_inputs(seed=0):
    import zlib

    import numpy as np

    out = dict(_drawn_inputs(seed))
    spreads = {}
    factors = {'L0_attn_Wqkv': 5.357, 'L0_attn_Wout': 5.332, 'L0_ffn_b1': 4.93, 'L0_ffn_b2': 3.541}
    for name, (base, spread) in spreads.items():
        noise = np.random.default_rng([zlib.crc32(name.encode()), seed]).standard_normal(out[name].shape)
        drawn = base * np.exp(spread * noise) if base else spread * noise
        out[name] = jnp.asarray(drawn.astype(out[name].dtype))
    for name, factor in factors.items():
        out[name] = (out[name] * factor).astype(out[name].dtype)
    return out
```

```python
from contextlib import ExitStack

import concourse.bass as bass
from concourse import mybir

F32 = mybir.dt.float32
F32R = mybir.dt.float32r
ALU = mybir.AluOpType
ACT = mybir.ActivationFunctionType
AX = mybir.AxisListType

P = 128
H = 16
HD = 16
SEG = 512
DIL = 8
BLOCK_M = 64
KEYS = SEG // DIL
T = SEG // P
NB = SEG // BLOCK_M
PB = P // NB
PAIRS = H // 2
PW = 2 * HD
PR = 3 * PW
QUADS = 2
D = H * HD
DH = D // P
EPS = 1e-5
GUARD = 1e-10


def ln_attention_ffn(nc, x, wq_t, wkv_t, wout_t, w1, b1, w2, b2, out):
    NSEG = x.shape[0] * x.shape[1] // SEG
    INTER = w1.shape[1]
    NH = INTER // P
    SCALE = float(HD) ** -0.5
    HBUF = 4
    LAG = 2
    RP = 4
    YB = 2
    PAIR_ORDER = [half * (PAIRS // 2) + j for j in range(PAIRS // 2) for half in range(DH)]
    PACKED = 16 * 3
    assert D == 256 and x.shape[2] == D and NSEG % 2 == 0 and NH == PAIRS and 2 * KEYS == P
    assert T == 4 and PB * NB == P

    x_rows = x.rearrange("b (s p t) d -> (b s) p t d", p=P, t=T)
    out_rows = out.rearrange("b (s p t) d -> (b s) p t d", p=P, t=T)

    with ExitStack() as ctx:
        def sb(name, shape, dt):
            return ctx.enter_context(nc.sbuf_tensor(name, shape, dt))

        def sem(name):
            return ctx.enter_context(nc.semaphore(name))

        identity = sb("identity", [P, P], F32)
        kv_mask = sb("kv_mask", [P, 2 * D], F32)
        head_ones = sb("head_ones", [P, PW], F32)
        minus_half = sb("minus_half", [P, T], F32)
        eps = sb("eps", [P, T], F32)
        b1_cols = sb("b1_cols", [P, NH], F32)
        b2_rows = sb("b2_rows", [P, D], F32)
        wq = [sb(f"wq_{n}", [P, DH, D], F32R) for n in ("hi", "lo")]
        wkv = [sb(f"wkv_{n}", [P, DH, 2 * D], F32R) for n in ("hi", "lo")]
        wout = [sb(f"wout_{n}", [P, DH, D], F32R) for n in ("hi", "lo")]
        w1s = [sb(f"w1_{n}", [P, DH, INTER], F32R) for n in ("hi", "lo")]
        w2s = [sb(f"w2_{n}", [P, NH, D], F32R) for n in ("hi", "lo")]
        x_raw = sb("x_raw", [P, 2, T, D], F32)
        x_b2 = sb("x_b2", [P, 2, T, D], F32)
        stats = sb("stats", [P, T, 6], F32)
        mean_var = sb("mean_var", [P, T, 2], F32)
        var_eps = sb("var_eps", [P, T], F32)
        rstd = sb("rstd", [P, T], F32)
        xn = sb("xn", [P, T, D], F32)
        xt = [sb(f"xt_{n}", [P, 2, DH, SEG], F32R) for n in ("hi", "lo")]
        xkey = [sb(f"xkey_{n}", [P, DH, P], F32R) for n in ("hi", "lo")]
        q_part = [sb(f"q_{n}", [P, DH, SEG], F32R) for n in ("hi", "lo")]
        q_pack = sb("q_pack", [P, PAIRS, SEG], F32R)
        kv = sb("kv", [P, 2, 2 * D], F32)
        k_split = sb("k_split", [P, PAIRS, 3, PW], F32R)
        k_pack = sb("k_pack", [P, PAIRS, P], F32R)
        s_max = sb("s_max", [P, PAIRS, NB], F32)
        w_exp = sb("w_exp", [P, PAIRS, SEG], F32)
        num = sb("num", [P, QUADS, SEG], F32)
        den = sb("den", [P, QUADS, SEG], F32)
        att = sb("att", [P, QUADS, SEG], F32)
        att_part = [sb(f"att_{n}", [P, 2, QUADS, SEG], F32R) for n in ("hi", "lo")]
        h_full = sb("h_full", [P, HBUF, SEG], F32)
        h_part = [sb(f"h_{n}", [P, HBUF, SEG], F32R) for n in ("hi", "lo")]
        y = sb("y", [P, 2, T, D], F32)
        w1_raw = w_exp[:].rearrange("p a b -> p (a b)")[:, 0:DH * INTER].rearrange("p (c n) -> p c n", c=DH)
        w2_raw = w_exp[:].rearrange("p a b -> p (a b)")[:, DH * INTER:].rearrange("p (c n) -> p c n", c=NH)
        wkv_raw = y[:].rearrange("p a b c -> p (a b c)")[:, 0:2 * DH * D].rearrange("p (c n) -> p c n", c=DH)
        wq_raw = y[:].rearrange("p a b c -> p (a b c)")[:, 2 * DH * D:3 * DH * D].rearrange("p (c n) -> p c n", c=DH)
        wout_raw = y[:].rearrange("p a b c -> p (a b c)")[:, 3 * DH * D:].rearrange("p (c n) -> p c n", c=DH)

        def bank(name):
            return ctx.enter_context(nc.psum_tensor(name, [P, SEG], F32))
        misc = [bank(f"misc{i}") for i in range(2)]
        h_bank = [bank(f"h_bank{i}") for i in range(2)]
        s_bank = [bank(f"s_bank{i}") for i in range(2)]
        y_bank = [bank(f"y_bank{i}") for i in range(YB)]

        const_loaded = sem("const_loaded")
        wqkv_loaded = sem("wqkv_loaded")
        w1_loaded = sem("w1_loaded")
        w2_loaded = sem("w2_loaded")
        identity_zero = sem("identity_zero")
        consts_made = sem("consts_made")
        masks_zero = sem("masks_zero")
        masks_made = sem("masks_made")
        w_hi = sem("w_hi")
        w_lo = sem("w_lo")
        x_loaded = [sem(f"x_loaded{i}") for i in range(2)]
        x_b2_ready = sem("x_b2_ready")
        stats_part = sem("stats_part")
        stats_ready = sem("stats_ready")
        var_ready = sem("var_ready")
        rstd_ready = sem("rstd_ready")
        xn_ready = sem("xn_ready")
        xt_psum = sem("xt_psum")
        xt_hi = sem("xt_hi")
        xt_lo = sem("xt_lo")
        xkey_hi = sem("xkey_hi")
        xkey_lo = sem("xkey_lo")
        q_psum = sem("q_psum")
        q_hi = sem("q_hi")
        q_lo = sem("q_lo")
        pair_packed = [sem(f"pair_packed{j}") for j in range(PAIRS // 2)]
        kv_psum = sem("kv_psum")
        kv_ready = sem("kv_ready")
        k_hi = sem("k_hi")
        k_lo = sem("k_lo")
        kt_psum = sem("kt_psum")
        k_packed = sem("k_packed")
        s_psum = sem("s_psum")
        max_ready = sem("max_ready")
        s_shifted = sem("s_shifted")
        w_ready = sem("w_ready")
        pv_psum = sem("pv_psum")
        num_ready = sem("num_ready")
        den_ready = sem("den_ready")
        rden_ready = sem("rden_ready")
        att_ready = sem("att_ready")
        att_hi = sem("att_hi")
        att_lo = sem("att_lo")
        h_psum = sem("h_psum")
        h_ready = sem("h_ready")
        h_hi = sem("h_hi")
        h_lo = sem("h_lo")
        h_used = sem("h_used")
        y_psum = sem("y_psum")
        y_ready = sem("y_ready")
        y_stored = [sem(f"y_stored{i}") for i in range(2)]

        def past(count):
            return max(count, 0) if isinstance(count, int) else count

        def iterations(eng, step):
            def fixed(s):
                step(s, s % 2, s >= 0, 0 <= s + 1 < NSEG, s + 2 < NSEG, s + 3 < NSEG)

            for s in range(-2, 2):
                fixed(s)
            with eng.Fori(1, NSEG // 2 - 2) as half:
                step(half * 2, 0, True, True, True, True)
                step(half * 2 + 1, 1, True, True, True, True)
            for s in range(NSEG - 4, NSEG):
                fixed(s)

        splits = [(wkv_raw, wkv, wqkv_loaded, 32), (wq_raw, wq, wqkv_loaded, 32), (w1_raw, w1s, w1_loaded, 16),
                  (w2_raw, w2s, w2_loaded, 32), (wout_raw, wout, w2_loaded, 32)]

        def f32(tile):
            return tile.bitcast(F32)

        block = ctx.enter_context(nc.Block())

        @block.sync
        def _(sp):
            def load_x(seg, par):
                sp.dma_start(x_raw[:, par], x_rows[seg]).then_inc(x_loaded[par], 16)

            def step(s, par, ffn, attention, norm, load):
                if isinstance(s, int) and s == -2:
                    load_x(0, 0)
                if isinstance(s, int) and s == -2:
                    sp.dma_start(wq_raw, wq_t.rearrange("(c p) n -> p c n", p=P)).then_inc(wqkv_loaded, 16)
                    sp.dma_start(wkv_raw, wkv_t.rearrange("(c p) n -> p c n", p=P)).then_inc(wqkv_loaded, 16)
                    sp.dma_start(w1_raw, w1.rearrange("(c p) n -> p c n", p=P)).then_inc(w1_loaded, 16)
                    sp.dma_start(w2_raw, w2.rearrange("(c p) n -> p c n", p=P)).then_inc(w2_loaded, 16)
                    sp.dma_start(wout_raw, wout_t.rearrange("(c p) n -> p c n", p=P)).then_inc(w2_loaded, 16)
                    sp.dma_start(b1_cols[:], b1).then_inc(const_loaded, 16)
                    sp.dma_start(b2_rows[:], b2.partition_broadcast(P)).then_inc(const_loaded, 16)
                if load:
                    sp.wait_ge(x_b2_ready, past(s + 2))
                    sp.wait_ge(xn_ready, past(s + 2))
                    load_x(s + 3, 1 - par)
                if norm:
                    sp.wait_ge(q_hi, (s + 3) * DH)
                    sp.wait_ge(q_lo, (s + 3) * DH)
                    for j in range(PAIRS // 2):
                        for r, part in enumerate((0, 1, 0)):
                            sp.dma_start(f32(q_pack[PW * r:PW * (r + 1), j::PAIRS // 2, :]),
                                         f32(q_part[part][PW * j:PW * (j + 1)])).then_inc(pair_packed[j], 16)
                if ffn:
                    sp.wait_ge(y_ready, (s + 1) * YB)
                    sp.dma_start(out_rows[s], y[:, par]).then_inc(y_stored[par], 16)

            iterations(sp, step)
            for par in range(2):
                sp.wait_ge(y_stored[par], 16 * (NSEG // 2))

        @block.gpsimd
        def _(pool):
            pool.memset(minus_half[:], -0.5).then_inc(consts_made, 1)
            pool.memset(eps[:], EPS).then_inc(consts_made, 1)
            pool.memset(identity[:], 0.0).then_inc(identity_zero, 1)
            pool.wait_ge(identity_zero, 1)
            pool.affine_select(out=identity[:], in_=identity[:], compare_op=ALU.not_equal, fill=1.0,
                               base=0, pattern=[[-1, P]], channel_multiplier=1).then_inc(consts_made, 1)

            def inverse_deviation(s):
                pool.wait_ge(stats_ready, s + 1)
                pool.wait_ge(xn_ready, past(s))
                pool.wait_ge(consts_made, 3)
                pool.tensor_tensor(var_eps[:], mean_var[:, :, 1], eps[:], ALU.add).then_inc(var_ready, 1)
                pool.wait_ge(var_ready, s + 1)
                pool.tensor_tensor(rstd[:], var_eps[:], minus_half[:], ALU.pow).then_inc(rstd_ready, 1)

            def hidden_lo(s, i):
                n = s * NH + i
                pool.wait_ge(h_ready, n + 1)
                pool.wait_ge(h_hi, n + 1)
                pool.wait_ge(h_used, past(n - HBUF + 1))
                pool.tensor_tensor(h_part[1][:, i % HBUF], h_full[:, i % HBUF], f32(h_part[0][:, i % HBUF]),
                                   ALU.subtract).then_inc(h_lo, 1)

            def attention_out(s, quad):
                pool.wait_ge(rden_ready, (s * QUADS + quad + 1) * (RP // QUADS))
                pool.wait_ge(num_ready, s * QUADS + quad + 1)
                pool.wait_ge(att_hi, past((s - 1) * QUADS + quad + 1))
                pool.tensor_tensor(att[:, quad], num[:, quad], den[:, quad], ALU.mult).then_inc(att_ready, 1)

            def attention_lo(s, quad, par):
                pool.wait_ge(att_ready, s * QUADS + quad + 1)
                pool.wait_ge(att_hi, s * QUADS + quad + 1)
                pool.tensor_tensor(att_part[1][:, par, quad], att[:, quad], f32(att_part[0][:, par, quad]),
                                   ALU.subtract).then_inc(att_lo, 1)

            def residual(s, par):
                if isinstance(s, int) and s == -1:
                    pool.wait_ge(const_loaded, 32)
                pool.wait_ge(x_loaded[1 - par], residual_loads(s, par))
                pool.wait_ge(y_ready, past(s * YB))
                pool.tensor_tensor(x_b2[:, 1 - par], x_raw[:, 1 - par],
                                   b2_rows[:].unsqueeze(1).to_broadcast([P, T, D]), ALU.add).then_inc(x_b2_ready, 1)

            def residual_loads(s, par):
                return (s + 1 - (1 - par)) * 8 + 16

            def step(s, par, ffn, attention, norm, load):
                for i in range(LAG, NH):
                    if ffn:
                        hidden_lo(s, i)
                    if i == 2 and attention:
                        residual(s, par)
                    if i in (4, 6) and ffn:
                        attention_out(s, i // 2 - 2)
                    if i in (5, 7) and ffn:
                        attention_lo(s, i // 2 - 2, par)
                if attention:
                    for i in range(LAG):
                        hidden_lo(s + 1, i)
                if load:
                    inverse_deviation(s + 3)

            inverse_deviation(0)
            iterations(pool, step)

        @block.scalar
        def _(act):
            def split_hi(n):
                raw, parts, loaded, count = splits[n]
                act.wait_ge(loaded, count)
                act.copy(parts[0][:], raw).then_inc(w_hi, 1)

            def hidden(s, i):
                n = s * NH + i
                if isinstance(n, int) and n == 0:
                    act.wait_ge(const_loaded, 32)
                act.wait_ge(h_psum, n + 1)
                act.wait_ge(h_lo, past(n - HBUF + 1))
                act.wait_ge(h_used, past(n - HBUF + 1))
                act.activation(h_part[0][:, i % HBUF], h_bank[i % 2][:], ACT.Relu,
                               bias=b1_cols[:, i:i + 1]).then_inc(h_hi, 1)
                act.activation(h_full[:, i % HBUF], h_bank[i % 2][:], ACT.Relu,
                               bias=b1_cols[:, i:i + 1]).then_inc(h_ready, 1)

            def exponential(s, n):
                pair = PAIR_ORDER[n]
                act.wait_ge(s_shifted, (s + 1) * PAIRS + n + 1)
                act.activation(w_exp[:, pair], w_exp[:, pair], ACT.Exp).then_inc(w_ready, 1)

            def attention_hi(s, quad, par):
                act.wait_ge(att_ready, s * QUADS + quad + 1)
                act.wait_ge(y_psum, past((s - 1) * YB))
                act.copy(att_part[0][:, par, quad], att[:, quad]).then_inc(att_hi, 1)

            def attention_drain(s, quad):
                n = (s + 1) * QUADS + quad + 1
                act.wait_ge(pv_psum, n)
                act.wait_ge(att_ready, past(n - QUADS))
                act.copy(num[:, quad], misc[0][:]).then_inc(num_ready, 1)
                act.add(den[:, quad], misc[1][:], GUARD).then_inc(den_ready, 1)

            def step(s, par, ffn, attention, norm, load):
                if isinstance(s, int) and s == -1:
                    for n in range(2, len(splits)):
                        split_hi(n)
                for i in range(LAG, NH - 1):
                    if attention:
                        exponential(s, i - LAG)
                    if ffn:
                        hidden(s, i)
                        if i == 5:
                            attention_hi(s, 0, par)
                if norm:
                    act.wait_ge(h_psum, past((s + 1) * NH))
                    for c in range(DH):
                        act.wait_ge(xt_psum, (s + 2) * DH + c + 1)
                        act.copy(xt[0][:, par, c], misc[c][:]).then_inc(xt_hi, 1)
                        act.copy(xkey[0][:, c].rearrange("p (a k) -> p a k", a=2),
                                 misc[c][:, 0:P:2].unsqueeze(1).to_broadcast([P, 2, KEYS])).then_inc(xkey_hi, 1)
                if ffn:
                    hidden(s, NH - 1)
                if attention:
                    exponential(s, PAIRS - 3)
                if ffn:
                    attention_hi(s, 1, par)
                if attention:
                    exponential(s, PAIRS - 2)
                    exponential(s, PAIRS - 1)
                if norm:
                    act.wait_ge(kv_ready, s + 3)
                    act.copy(k_split[:, :, 0:2], kv[:, par, 0:D].rearrange("p (a d) -> p a d", a=PAIRS)
                             .unsqueeze(2).to_broadcast([P, PAIRS, 2, PW])).then_inc(k_hi, 1)
                    for m in range(DH):
                        act.wait_ge(q_psum, (s + 2) * DH + m + 1)
                        act.copy(q_part[0][:, m], h_bank[m][:]).then_inc(q_hi, 1)
                if attention:
                    attention_drain(s, 0)
                if norm:
                    for quad in range(QUADS):
                        act.wait_ge(kt_psum, (s + 2) * QUADS + quad + 1)
                        act.copy(k_pack[0:PR, 4 * quad:4 * quad + 4].rearrange("p a k -> p (a k)"),
                                 s_bank[quad][0:PR]).then_inc(k_packed, 1)
                if attention:
                    for i in range(LAG):
                        hidden(s + 1, i)
                    attention_drain(s, 1)

            for n in range(2):
                split_hi(n)
            iterations(act, step)

        @block.vector
        def _(dve):
            def split_lo(n):
                raw, parts, loaded, count = splits[n]
                dve.wait_ge(loaded, count)
                dve.wait_ge(w_hi, n + 1)
                dve.tensor_tensor(parts[1][:], raw, f32(parts[0][:]), ALU.subtract).then_inc(w_lo, 1)

            dve.memset(kv_mask[:], 0.0).then_inc(masks_zero, 1)
            dve.memset(head_ones[:], 0.0).then_inc(masks_zero, 1)
            dve.wait_ge(masks_zero, 2)
            mask = kv_mask[:].rearrange("p (w a b d) -> p w a b d", w=2, a=PAIRS, b=2)
            for b in range(2):
                rows = slice(b * KEYS, (b + 1) * KEYS)
                dve.memset(mask[rows, 0, :, b, :], SCALE).then_inc(masks_made, 1)
                dve.memset(mask[rows, 1, :, b, :], 1.0).then_inc(masks_made, 1)
                dve.memset(head_ones[rows, b * HD:(b + 1) * HD], 1.0).then_inc(masks_made, 1)

            def statistics(s, par):
                dve.wait_ge(x_loaded[par], (s - par) * 8 + 16)
                for t in range(T):
                    op = dve.bn_stats(stats[:, t], x_raw[:, par, t])
                op.then_inc(stats_part, 1)

            def mean_variance(s):
                for t in range(T):
                    op = dve.bn_aggr(mean_var[:, t], stats[:, t])
                op.then_inc(stats_ready, 1)

            def statistics_done(s):
                dve.wait_ge(stats_part, s + 1)
                dve.wait_ge(var_ready, past(s))

            def normalise(s, par):
                dve.wait_ge(stats_ready, s + 1)
                dve.wait_ge(rstd_ready, s + 1)
                dve.wait_ge(xt_psum, past(s * DH))
                for t in range(T):
                    op = dve.tensor_scalar(xn[:, t], x_raw[:, par, t], mean_var[:, t, 0:1], rstd[:, t:t + 1],
                                           ALU.subtract, ALU.mult)
                op.then_inc(xn_ready, 1)

            def shift_scores(s, n):
                pair = PAIR_ORDER[n]
                ps = s_bank[n % 2][:].rearrange("p (t n i) -> p t n i", t=T, n=NB)
                dve.wait_ge(s_psum, (s + 1) * PAIRS + n + 1)
                dve.tensor_reduce(s_max[:, pair], ps.rearrange("p t n i -> p n t i"), AX.XY,
                                  ALU.max).then_inc(max_ready, 1)
                if n == 0:
                    dve.wait_ge(pv_psum, past((s + 1) * QUADS))
                dve.wait_ge(max_ready, (s + 1) * PAIRS + n + 1)
                top = s_max[:, pair].unsqueeze(1).unsqueeze(3).to_broadcast([P, T, NB, PB])
                dve.tensor_tensor(w_exp[:, pair].rearrange("p (t n i) -> p t n i", t=T, n=NB), ps, top,
                                  ALU.subtract).then_inc(s_shifted, 1)

            def invert_den(s, part):
                quad, n = part // (RP // QUADS), part % (RP // QUADS)
                columns = slice(n * SEG * QUADS // RP, (n + 1) * SEG * QUADS // RP)
                dve.wait_ge(den_ready, s * QUADS + quad + 1)
                dve.reciprocal(den[:, quad, columns], den[:, quad, columns]).then_inc(rden_ready, 1)

            def transposed_lo(s, par):
                for c in range(DH):
                    dve.wait_ge(xt_hi, (s + 2) * DH + c + 1)
                    dve.wait_ge(xkey_hi, (s + 2) * DH + c + 1)
                    dve.tensor_tensor(xt[1][:, par, c], misc[c][:], f32(xt[0][:, par, c]),
                                      ALU.subtract).then_inc(xt_lo, 1)
                    dve.tensor_tensor(xkey[1][:, c].rearrange("p (a k) -> p a k", a=2),
                                      misc[c][:, 0:P:2].unsqueeze(1).to_broadcast([P, 2, KEYS]),
                                      f32(xkey[0][:, c]).rearrange("p (a k) -> p a k", a=2),
                                      ALU.subtract).then_inc(xkey_lo, 1)

            def project_in(s, par):
                if isinstance(s, int) and s == -2:
                    dve.wait_ge(masks_made, 6)
                dve.wait_ge(kv_psum, s + 3)
                dve.tensor_tensor(kv[:, par], misc[0][:], kv_mask[:], ALU.mult).then_inc(kv_ready, 1)
                dve.wait_ge(kv_ready, s + 3)
                dve.wait_ge(k_hi, s + 3)
                dve.tensor_tensor(k_split[:, :, 2], kv[:, par, 0:D].rearrange("p (a d) -> p a d", a=PAIRS),
                                  f32(k_split[:, :, 0]), ALU.subtract).then_inc(k_lo, 1)
                for m in range(DH):
                    dve.wait_ge(q_hi, (s + 2) * DH + m + 1)
                    dve.tensor_tensor(q_part[1][:, m], h_bank[m][:], f32(q_part[0][:, m]),
                                      ALU.subtract).then_inc(q_lo, 1)

            def step(s, par, ffn, attention, norm, load):
                if isinstance(s, int) and s == -1:
                    for n in range(2, len(splits)):
                        split_lo(n)
                for n in range(PAIRS):
                    if n == 6 and norm:
                        transposed_lo(s, par)
                    if attention:
                        shift_scores(s, n)
                    if n == 1 and norm:
                        normalise(s + 2, par)
                    if n in (2, 4) and ffn:
                        invert_den(s, RP // QUADS + n // 2 - 1)
                if norm:
                    project_in(s, par)
                if attention:
                    invert_den(s + 1, 0)
                if load:
                    statistics(s + 3, 1 - par)
                    statistics_done(s + 3)
                if attention:
                    invert_den(s + 1, 1)
                if load:
                    mean_variance(s + 3)
                if ffn:
                    dve.wait_ge(x_b2_ready, s + 1)
                    dve.wait_ge(y_stored[par], past((s - par) * 8))
                    for b in range(YB):
                        dve.wait_ge(y_psum, s * YB + b + 1)
                        dve.tensor_tensor(y[:, par, 2 * b:2 * b + 2],
                                          y_bank[b][:].rearrange("p (t d) -> p t d", t=2),
                                          x_b2[:, par, 2 * b:2 * b + 2], ALU.add).then_inc(y_ready, 1)

            statistics(0, 0)
            statistics_done(0)
            mean_variance(0)
            for n in range(2):
                split_lo(n)
            iterations(dve, step)

        @block.tensor
        def _(pe):
            def three_products(ps, pairs, start, stop, alone=True):
                for c, (stationary, moving) in enumerate(pairs):
                    for n, (a, b) in enumerate(((0, 0), (0, 1), (1, 0))):
                        mm = pe.matmul(ps, stationary[a], moving[b], start=start and c == 0 and n == 0,
                                       stop=stop and c == len(pairs) - 1 and n == 2, skip_group_check=not alone)
                return mm

            def first_product(s, i, par, attention=True):
                n = s * NH + i
                if isinstance(n, int) and n == 0:
                    pe.wait_ge(w_lo, 3)
                if i < 2 and attention:
                    pe.wait_ge(q_lo, (s + 1) * DH + i + 1)
                elif i >= 2:
                    pe.wait_ge(h_ready, n - 1)
                three_products(h_bank[i % 2][:],
                               [([w[:, c, i * P:(i + 1) * P] for w in w1s], [x_[:, par, c] for x_ in xt])
                                for c in range(DH)], True, True).then_inc(h_psum, 1)

            def second_product(s, i):
                n = s * NH + i
                if isinstance(s, int) and s == 0 and i == 0:
                    pe.wait_ge(w_lo, len(splits))
                pe.wait_ge(h_hi, n + 1)
                pe.wait_ge(h_lo, n + 1)
                for t in range(T):
                    if i == 0 and t % 2 == 0:
                        pe.wait_ge(y_ready, past((s - 1) * YB + t // 2 + 1))
                    mm = three_products(y_bank[t // 2][:, (t % 2) * D:(t % 2 + 1) * D],
                                        [([h[:, i % HBUF, t * P:(t + 1) * P] for h in h_part],
                                          [w[:, i, :] for w in w2s])], i == 0 and t % 2 == 0, False, alone=False)
                mm.then_inc(h_used, 1)

            def output_product(s, par):
                pe.wait_ge(att_hi, (s + 1) * QUADS)
                pe.wait_ge(att_lo, (s + 1) * QUADS)
                for t in range(T):
                    mm = three_products(y_bank[t // 2][:, (t % 2) * D:(t % 2 + 1) * D],
                                        [([a[:, par, m, t * P:(t + 1) * P] for a in att_part],
                                          [w[:, m, :] for w in wout]) for m in range(DH)],
                                        False, t % 2 == 1, alone=False)
                    if t % 2 == 1:
                        mm.then_inc(y_psum, 1)

            def scores(s, n):
                pair = PAIR_ORDER[n]
                if n % 2 == 0:
                    pe.wait_ge(pair_packed[n // 2], (s + 2) * PACKED)
                pe.wait_ge(s_shifted, past((s + 1) * PAIRS + n - 1))
                if n < 2:
                    pe.wait_ge(k_packed, (s + 2) * QUADS)
                pe.matmul(s_bank[n % 2][:], k_pack[0:PR, pair], q_pack[0:PR, pair], start=True,
                          stop=True).then_inc(s_psum, 1)

            def transpose_x(s, first):
                pe.wait_ge(xn_ready, s + 3)
                if isinstance(s, int) and s == -2:
                    pe.wait_ge(consts_made, 3)
                for c in range(DH):
                    pe.wait_ge((num_ready, den_ready)[c], past((s + 1) * QUADS))
                    if first:
                        pe.wait_ge((kv_ready, xt_lo)[c], past((s + 2) * (1, DH)[c]))
                    for t in range(T):
                        mm = pe.transpose(misc[c][:, t * P:(t + 1) * P], xn[:, t, c * P:(c + 1) * P], identity[:])
                    mm.then_inc(xt_psum, 1)

            def keys_values(s, par):
                if isinstance(s, int) and s == -2:
                    pe.wait_ge(w_lo, 2)
                for ready in (xt_hi, xt_lo, xkey_hi, xkey_lo):
                    pe.wait_ge(ready, (s + 3) * DH)
                three_products(misc[0][:], [([k[:, c] for k in xkey], [w[:, c] for w in wkv]) for c in range(DH)],
                               True, True).then_inc(kv_psum, 1)

            def transpose_k(s):
                pe.wait_ge(k_hi, s + 3)
                pe.wait_ge(k_lo, s + 3)
                pe.wait_ge(s_shifted, past((s + 2) * PAIRS))
                for quad in range(QUADS):
                    for j in range(PAIRS // QUADS):
                        pair = quad * (PAIRS // QUADS) + j
                        mm = pe.transpose(s_bank[quad][0:PR, j * P:(j + 1) * P],
                                          f32(k_split[:, pair]).rearrange("p a d -> p (a d)"), identity[:])
                    mm.then_inc(kt_psum, 1)

            def queries(s, par):
                for m in range(DH):
                    pe.wait_ge(h_ready, past(s * NH + NH - 1 + m))
                    three_products(h_bank[m][:], [([w[:, c, m * P:(m + 1) * P] for w in wq],
                                                   [x_[:, par, c] for x_ in xt]) for c in range(DH)],
                                   True, True).then_inc(q_psum, 1)

            def weighted_values(s, quad, par, norm):
                pe.wait_ge(w_ready, (s + 1) * PAIRS + PAIRS - (QUADS - 1 - quad))
                for b, (drained, stationary) in enumerate((
                        (num_ready, lambda p: kv[:, 1 - par, D + 32 * p:D + 32 * p + 32]),
                        (den_ready, lambda p: head_ones[:]))):
                    if quad == 0 and norm:
                        pe.wait_ge(kv_ready, s + 3)
                        pe.wait_ge(xt_lo, (s + 3) * DH)
                    else:
                        pe.wait_ge(drained, (s + 1) * QUADS + quad)
                    for j in range(PAIRS // QUADS):
                        pair = quad * (PAIRS // QUADS) + j
                        mm = pe.matmul(misc[b][32 * j:32 * j + 32, :], stationary(pair), w_exp[:, pair],
                                       start=True, stop=True)
                mm.then_inc(pv_psum, 1)

            def step(s, par, ffn, attention, norm, load):
                for i in range(LAG, NH):
                    if attention:
                        scores(s, i - LAG)
                    if i == NH - 1 and norm:
                        transpose_x(s, not ffn)
                    if ffn:
                        first_product(s, i, par)
                        second_product(s, i - LAG)
                if attention:
                    scores(s, PAIRS - 2)
                if ffn:
                    second_product(s, NH - 2)
                if attention:
                    scores(s, PAIRS - 1)
                if norm:
                    keys_values(s, par)
                    queries(s, par)
                if ffn:
                    second_product(s, NH - 1)
                if attention:
                    weighted_values(s, 0, par, norm)
                if norm:
                    transpose_k(s)
                if attention:
                    for i in range(LAG):
                        first_product(s + 1, i, 1 - par, norm)
                    weighted_values(s, 1, par, norm)
                if ffn:
                    output_product(s, par)

            iterations(pe, step)


def kernel(L0_attn_x, L0_attn_Wqkv, L0_attn_Wout, L0_ffn_W1, L0_ffn_b1, L0_ffn_W2, L0_ffn_b2):
    import numpy as np
    import concourse.bacc as bacc
    from concourse.bass_utils import run_bass_kernel_spmd

    wqkv = np.asarray(L0_attn_Wqkv)
    arrays = {
        "x": np.asarray(L0_attn_x),
        "wq_t": wqkv[:D].T,
        "wkv_t": wqkv[D:].T,
        "wout_t": np.asarray(L0_attn_Wout).T,
        "w1": np.asarray(L0_ffn_W1),
        "b1": np.asarray(L0_ffn_b1).reshape(-1, P).T,
        "w2": np.asarray(L0_ffn_W2),
        "b2": np.asarray(L0_ffn_b2),
    }
    arrays = {name: np.ascontiguousarray(a) for name, a in arrays.items()}
    nc = bacc.Bacc("TRN2", target_bir_lowering=False, num_devices=1)
    args = [nc.dram_tensor(name, a.shape, mybir.dt.from_np(a.dtype), kind="ExternalInput").ap()
            for name, a in arrays.items()]
    out = nc.dram_tensor("out", arrays["x"].shape, F32, kind="ExternalOutput").ap()
    ln_attention_ffn(nc, *args, out)
    r = run_bass_kernel_spmd(nc, [arrays], core_ids=[0])
    return r.results[0]["out"]
```

```python
from contextlib import ExitStack

import concourse.bass as bass
from concourse import mybir

F32 = mybir.dt.float32
F32R = mybir.dt.float32r
ALU = mybir.AluOpType
ACT = mybir.ActivationFunctionType
AX = mybir.AxisListType

P = 128
H = 16
HD = 16
SEG = 512
DIL = 8
BLOCK_M = 64
KEYS = SEG // DIL
T = SEG // P
NB = SEG // BLOCK_M
PB = P // NB
PAIRS = H // 2
PW = 2 * HD
PR = 3 * PW
QUADS = 2
D = H * HD
DH = D // P
EPS = 1e-5
GUARD = 1e-10


def ln_attention_ffn(nc, x, wq_t, wkv_t, wout_t, w1, b1, w2, b2, out):
    NSEG = x.shape[0] * x.shape[1] // SEG
    INTER = w1.shape[1]
    NH = INTER // P
    SCALE = float(HD) ** -0.5
    HBUF = 4
    LAG = 2
    EARLY = 5
    RP = 4
    YB = 2
    PAIR_ORDER = [half * (PAIRS // 2) + j for j in range(PAIRS // 2) for half in range(DH)]
    PACKED = 16 * 6
    assert D == 256 and x.shape[2] == D and NSEG % 2 == 0 and NH == PAIRS and 2 * KEYS == P
    assert T == 4 and PB * NB == P

    x_rows = x.rearrange("b (s p t) d -> (b s) p t d", p=P, t=T)
    out_rows = out.rearrange("b (s p t) d -> (b s) p t d", p=P, t=T)

    with ExitStack() as ctx:
        def sb(name, shape, dt):
            return ctx.enter_context(nc.sbuf_tensor(name, shape, dt))

        def sem(name):
            return ctx.enter_context(nc.semaphore(name))

        identity = sb("identity", [P, P], F32)
        kv_mask = sb("kv_mask", [P, 2 * D], F32)
        head_ones = sb("head_ones", [P, PW], F32)
        minus_half = sb("minus_half", [P, T], F32)
        eps = sb("eps", [P, T], F32)
        b1_cols = sb("b1_cols", [P, NH], F32)
        b2_rows = sb("b2_rows", [P, D], F32)
        wq = [sb(f"wq_{n}", [P, DH, D], F32R) for n in ("hi", "lo")]
        wkv = [sb(f"wkv_{n}", [P, DH, 2 * D], F32R) for n in ("hi", "lo")]
        wout = [sb(f"wout_{n}", [P, DH, D], F32R) for n in ("hi", "lo")]
        w1s = [sb(f"w1_{n}", [P, DH, INTER], F32R) for n in ("hi", "lo")]
        w2s = [sb(f"w2_{n}", [P, NH, D], F32R) for n in ("hi", "lo")]
        x_raw = sb("x_raw", [P, 2, T, D], F32)
        x_b2 = sb("x_b2", [P, 2, T, D], F32)
        stats = sb("stats", [P, T, 6], F32)
        mean_var = sb("mean_var", [P, T, 2], F32)
        var_eps = sb("var_eps", [P, T], F32)
        rstd = sb("rstd", [P, T], F32)
        xn = sb("xn", [P, T, D], F32)
        xt = [sb(f"xt_{n}", [P, 2, DH, SEG], F32R) for n in ("hi", "lo")]
        xkey = [sb(f"xkey_{n}", [P, DH, P], F32R) for n in ("hi", "lo")]
        q_part = [sb(f"q_{n}", [P, DH, SEG], F32R) for n in ("hi", "lo")]
        q_pack = sb("q_pack", [P, PAIRS, SEG], F32R)
        kv = sb("kv", [P, 2, 2 * D], F32)
        k_part = [sb(f"k_{n}", [P, DH, P], F32R) for n in ("hi", "lo")]
        k_pack = sb("k_pack", [P, PAIRS, P], F32R)
        s_max = sb("s_max", [P, PAIRS, NB], F32)
        w_exp = sb("w_exp", [P, PAIRS, SEG], F32)
        num = sb("num", [P, QUADS, SEG], F32)
        den = sb("den", [P, QUADS, SEG], F32)
        att = sb("att", [P, QUADS, SEG], F32)
        att_part = [sb(f"att_{n}", [P, 2, QUADS, SEG], F32R) for n in ("hi", "lo")]
        h_full = sb("h_full", [P, HBUF, SEG], F32)
        h_part = [sb(f"h_{n}", [P, HBUF, SEG], F32R) for n in ("hi", "lo")]
        y = sb("y", [P, 2, T, D], F32)
        w1_raw = w_exp[:].rearrange("p a b -> p (a b)")[:, 0:DH * INTER].rearrange("p (c n) -> p c n", c=DH)
        w2_raw = w_exp[:].rearrange("p a b -> p (a b)")[:, DH * INTER:].rearrange("p (c n) -> p c n", c=NH)
        wkv_raw = y[:].rearrange("p a b c -> p (a b c)")[:, 0:2 * DH * D].rearrange("p (c n) -> p c n", c=DH)
        wq_raw = y[:].rearrange("p a b c -> p (a b c)")[:, 2 * DH * D:3 * DH * D].rearrange("p (c n) -> p c n", c=DH)
        wout_raw = y[:].rearrange("p a b c -> p (a b c)")[:, 3 * DH * D:].rearrange("p (c n) -> p c n", c=DH)

        def bank(name):
            return ctx.enter_context(nc.psum_tensor(name, [P, SEG], F32))
        misc = [bank(f"misc{i}") for i in range(2)]
        h_bank = [bank(f"h_bank{i}") for i in range(2)]
        s_bank = [bank(f"s_bank{i}") for i in range(2)]
        y_bank = [bank(f"y_bank{i}") for i in range(YB)]

        const_loaded = sem("const_loaded")
        wqkv_loaded = sem("wqkv_loaded")
        w1_loaded = sem("w1_loaded")
        w2_loaded = sem("w2_loaded")
        identity_zero = sem("identity_zero")
        consts_made = sem("consts_made")
        masks_zero = sem("masks_zero")
        masks_made = sem("masks_made")
        w_hi = sem("w_hi")
        w_lo = sem("w_lo")
        x_loaded = [sem(f"x_loaded{i}") for i in range(2)]
        x_b2_ready = sem("x_b2_ready")
        stats_part = sem("stats_part")
        stats_ready = sem("stats_ready")
        var_ready = sem("var_ready")
        rstd_ready = sem("rstd_ready")
        xn_ready = sem("xn_ready")
        xt_psum = sem("xt_psum")
        xt_hi = sem("xt_hi")
        xt_lo = sem("xt_lo")
        xkey_hi = sem("xkey_hi")
        xkey_lo = sem("xkey_lo")
        q_psum = sem("q_psum")
        q_hi = sem("q_hi")
        q_lo = sem("q_lo")
        pair_packed = [sem(f"pair_packed{j}") for j in range(PAIRS // 2)]
        kv_psum = sem("kv_psum")
        kv_ready = sem("kv_ready")
        k_hi = sem("k_hi")
        k_lo = sem("k_lo")
        kt_psum = sem("kt_psum")
        s_psum = sem("s_psum")
        max_ready = sem("max_ready")
        s_shifted = sem("s_shifted")
        w_ready = sem("w_ready")
        pv_psum = sem("pv_psum")
        num_ready = sem("num_ready")
        den_ready = sem("den_ready")
        rden_ready = sem("rden_ready")
        att_ready = sem("att_ready")
        att_hi = sem("att_hi")
        att_lo = sem("att_lo")
        h_psum = sem("h_psum")
        h_ready = sem("h_ready")
        h_hi = sem("h_hi")
        h_lo = sem("h_lo")
        h_used = sem("h_used")
        y_psum = sem("y_psum")
        y_ready = sem("y_ready")
        y_stored = [sem(f"y_stored{i}") for i in range(2)]

        def past(count):
            return max(count, 0) if isinstance(count, int) else count

        def iterations(eng, step):
            def fixed(s):
                step(s, s % 2, s >= 0, 0 <= s + 1 < NSEG, s + 2 < NSEG, s + 3 < NSEG)

            for s in range(-2, 2):
                fixed(s)
            with eng.Fori(1, NSEG // 2 - 2) as half:
                step(half * 2, 0, True, True, True, True)
                step(half * 2 + 1, 1, True, True, True, True)
            for s in range(NSEG - 4, NSEG):
                fixed(s)

        def tile_steps(s, ffn):
            if isinstance(s, int) and s == -1:
                return {i: i for i in range(LAG, EARLY)}, {i: i - LAG for i in range(LAG, EARLY)}
            if isinstance(s, int) and s == 0:
                return {LAG + 1 + i: EARLY + LAG + i for i in range(NH - EARLY - LAG)}, \
                       {LAG + 1 + i: EARLY - LAG + i for i in range(NH - EARLY)}
            if not ffn:
                return {}, {}
            return {i: i for i in range(LAG, NH)}, {i: i - LAG for i in range(LAG, NH)}

        def tail_tiles(s, attention):
            if isinstance(s, int) and s < 0:
                return 0, [(0, 1), (EARLY, EARLY + 1)][s + 2]
            return s + 1, (0, 1) if attention else ()

        splits = [(wkv_raw, wkv, wqkv_loaded, 32), (wq_raw, wq, wqkv_loaded, 32), (w1_raw, w1s, w1_loaded, 16),
                  (w2_raw, w2s, w2_loaded, 32), (wout_raw, wout, w2_loaded, 32)]

        def f32(tile):
            return tile.bitcast(F32)

        block = ctx.enter_context(nc.Block())

        @block.sync
        def _(sp):
            def load_x(seg, par):
                sp.dma_start(x_raw[:, par], x_rows[seg]).then_inc(x_loaded[par], 16)

            def step(s, par, ffn, attention, norm, load):
                if isinstance(s, int) and s == -2:
                    load_x(0, 0)
                if isinstance(s, int) and s == -2:
                    sp.dma_start(wq_raw, wq_t.rearrange("(c p) n -> p c n", p=P)).then_inc(wqkv_loaded, 16)
                    sp.dma_start(wkv_raw, wkv_t.rearrange("(c p) n -> p c n", p=P)).then_inc(wqkv_loaded, 16)
                    sp.dma_start(w1_raw, w1.rearrange("(c p) n -> p c n", p=P)).then_inc(w1_loaded, 16)
                    sp.dma_start(w2_raw, w2.rearrange("(c p) n -> p c n", p=P)).then_inc(w2_loaded, 16)
                    sp.dma_start(wout_raw, wout_t.rearrange("(c p) n -> p c n", p=P)).then_inc(w2_loaded, 16)
                    sp.dma_start(b1_cols[:], b1).then_inc(const_loaded, 16)
                    sp.dma_start(b2_rows[:], b2.partition_broadcast(P)).then_inc(const_loaded, 16)
                if load:
                    sp.wait_ge(x_b2_ready, past(s + 2))
                    sp.wait_ge(xn_ready, past(s + 2))
                    load_x(s + 3, 1 - par)
                if norm:
                    sp.wait_ge(q_hi, (s + 3) * DH)
                    sp.wait_ge(q_lo, (s + 3) * DH)
                    sp.wait_ge(k_hi, s + 3)
                    sp.wait_ge(k_lo, s + 3)
                    for j in range(PAIRS // 2):
                        for r, part in enumerate((0, 0, 1)):
                            sp.dma_start(f32(k_pack[PW * r:PW * (r + 1), j::PAIRS // 2, :]),
                                         f32(k_part[part][PW * j:PW * (j + 1)])).then_inc(pair_packed[j], 16)
                        for r, part in enumerate((0, 1, 0)):
                            sp.dma_start(f32(q_pack[PW * r:PW * (r + 1), j::PAIRS // 2, :]),
                                         f32(q_part[part][PW * j:PW * (j + 1)])).then_inc(pair_packed[j], 16)
                if ffn:
                    sp.wait_ge(y_ready, (s + 1) * YB)
                    sp.dma_start(out_rows[s], y[:, par]).then_inc(y_stored[par], 16)

            iterations(sp, step)
            for par in range(2):
                sp.wait_ge(y_stored[par], 16 * (NSEG // 2))

        @block.gpsimd
        def _(pool):
            pool.memset(minus_half[:], -0.5).then_inc(consts_made, 1)
            pool.memset(eps[:], EPS).then_inc(consts_made, 1)
            pool.memset(identity[:], 0.0).then_inc(identity_zero, 1)
            pool.wait_ge(identity_zero, 1)
            pool.affine_select(out=identity[:], in_=identity[:], compare_op=ALU.not_equal, fill=1.0,
                               base=0, pattern=[[-1, P]], channel_multiplier=1).then_inc(consts_made, 1)

            def inverse_deviation(s):
                pool.wait_ge(stats_ready, s + 1)
                pool.wait_ge(xn_ready, past(s))
                pool.wait_ge(consts_made, 3)
                pool.tensor_tensor(var_eps[:], mean_var[:, :, 1], eps[:], ALU.add).then_inc(var_ready, 1)
                pool.wait_ge(var_ready, s + 1)
                pool.tensor_tensor(rstd[:], var_eps[:], minus_half[:], ALU.pow).then_inc(rstd_ready, 1)

            def hidden_lo(s, i):
                n = s * NH + i
                pool.wait_ge(h_ready, n + 1)
                pool.wait_ge(h_hi, n + 1)
                pool.wait_ge(h_used, past(n - HBUF + 1))
                pool.tensor_tensor(h_part[1][:, i % HBUF], h_full[:, i % HBUF], f32(h_part[0][:, i % HBUF]),
                                   ALU.subtract).then_inc(h_lo, 1)

            def attention_out(s, quad):
                pool.wait_ge(rden_ready, (s * QUADS + quad + 1) * (RP // QUADS))
                pool.wait_ge(num_ready, s * QUADS + quad + 1)
                pool.wait_ge(att_hi, past((s - 1) * QUADS + quad + 1))
                pool.tensor_tensor(att[:, quad], num[:, quad], den[:, quad], ALU.mult).then_inc(att_ready, 1)

            def attention_lo(s, quad, par):
                pool.wait_ge(att_ready, s * QUADS + quad + 1)
                pool.wait_ge(att_hi, s * QUADS + quad + 1)
                pool.tensor_tensor(att_part[1][:, par, quad], att[:, quad], f32(att_part[0][:, par, quad]),
                                   ALU.subtract).then_inc(att_lo, 1)

            def residual(s, par):
                if isinstance(s, int) and s == -1:
                    pool.wait_ge(const_loaded, 32)
                pool.wait_ge(x_loaded[1 - par], residual_loads(s, par))
                pool.wait_ge(y_ready, past(s * YB))
                pool.tensor_tensor(x_b2[:, 1 - par], x_raw[:, 1 - par],
                                   b2_rows[:].unsqueeze(1).to_broadcast([P, T, D]), ALU.add).then_inc(x_b2_ready, 1)

            def residual_loads(s, par):
                return (s + 1 - (1 - par)) * 8 + 16

            def step(s, par, ffn, attention, norm, load):
                first, _ = tile_steps(s, ffn)
                for i in range(LAG, NH):
                    if i in first:
                        hidden_lo(past(s), first[i])
                    if i == 2 and attention:
                        residual(s, par)
                    if i in (4, 6) and ffn:
                        attention_out(s, i // 2 - 2)
                    if i in (5, 7) and ffn:
                        attention_lo(s, i // 2 - 2, par)
                segment, tiles = tail_tiles(s, attention)
                for i in tiles:
                    hidden_lo(segment, i)
                if load:
                    inverse_deviation(s + 3)

            inverse_deviation(0)
            iterations(pool, step)

        @block.scalar
        def _(act):
            def split_hi(n):
                raw, parts, loaded, count = splits[n]
                act.wait_ge(loaded, count)
                act.copy(parts[0][:], raw).then_inc(w_hi, 1)

            def hidden(s, i):
                n = s * NH + i
                if isinstance(n, int) and n == 0:
                    act.wait_ge(const_loaded, 32)
                act.wait_ge(h_psum, n + 1)
                act.wait_ge(h_lo, past(n - HBUF + 1))
                act.wait_ge(h_used, past(n - HBUF + 1))
                act.activation(h_part[0][:, i % HBUF], h_bank[i % 2][:], ACT.Relu,
                               bias=b1_cols[:, i:i + 1]).then_inc(h_hi, 1)
                act.activation(h_full[:, i % HBUF], h_bank[i % 2][:], ACT.Relu,
                               bias=b1_cols[:, i:i + 1]).then_inc(h_ready, 1)

            def exponential(s, n):
                pair = PAIR_ORDER[n]
                act.wait_ge(s_shifted, (s + 1) * PAIRS + n + 1)
                act.activation(w_exp[:, pair], w_exp[:, pair], ACT.Exp).then_inc(w_ready, 1)

            def attention_hi(s, quad, par):
                act.wait_ge(att_ready, s * QUADS + quad + 1)
                act.wait_ge(y_psum, past((s - 1) * YB))
                act.copy(att_part[0][:, par, quad], att[:, quad]).then_inc(att_hi, 1)

            def attention_drain(s, quad):
                n = (s + 1) * QUADS + quad + 1
                act.wait_ge(pv_psum, n)
                act.wait_ge(att_ready, past(n - QUADS))
                act.copy(num[:, quad], misc[0][:]).then_inc(num_ready, 1)
                act.add(den[:, quad], misc[1][:], GUARD).then_inc(den_ready, 1)

            def step(s, par, ffn, attention, norm, load):
                first, _ = tile_steps(s, ffn)
                for i in range(LAG, NH - 1):
                    if attention:
                        exponential(s, i - LAG)
                    if i in first:
                        hidden(past(s), first[i])
                    if i == 5 and ffn:
                        attention_hi(s, 0, par)
                if norm:
                    act.wait_ge(h_psum, past((s + 1) * NH))
                    for c in range(DH):
                        act.wait_ge(xt_psum, (s + 2) * DH + c + 1)
                        act.copy(xt[0][:, par, c], misc[c][:]).then_inc(xt_hi, 1)
                        act.copy(xkey[0][:, c].rearrange("p (a k) -> p a k", a=2),
                                 misc[c][:, 0:P:2].unsqueeze(1).to_broadcast([P, 2, KEYS])).then_inc(xkey_hi, 1)
                if isinstance(s, int) and s == -2:
                    split_hi(2)
                if NH - 1 in first:
                    hidden(s, NH - 1)
                if attention:
                    exponential(s, PAIRS - 3)
                if ffn:
                    attention_hi(s, 1, par)
                if attention:
                    exponential(s, PAIRS - 2)
                    exponential(s, PAIRS - 1)
                if norm:
                    for m in range(DH):
                        act.wait_ge(q_psum, (s + 2) * DH + m + 1)
                        act.copy(q_part[0][:, m], h_bank[m][:]).then_inc(q_hi, 1)
                    act.wait_ge(kt_psum, s + 3)
                    act.copy(k_part[0][:].rearrange("p c k -> p (c k)"), s_bank[0][:, 0:DH * P]).then_inc(k_hi, 1)
                if isinstance(s, int) and s == -2:
                    for n in range(3, len(splits)):
                        split_hi(n)
                if attention:
                    attention_drain(s, 0)
                segment, tiles = tail_tiles(s, attention)
                for i in tiles:
                    hidden(segment, i)
                if attention:
                    attention_drain(s, 1)

            for n in range(2):
                split_hi(n)
            iterations(act, step)

        @block.vector
        def _(dve):
            def split_lo(n):
                raw, parts, loaded, count = splits[n]
                dve.wait_ge(loaded, count)
                dve.wait_ge(w_hi, n + 1)
                dve.tensor_tensor(parts[1][:], raw, f32(parts[0][:]), ALU.subtract).then_inc(w_lo, 1)

            dve.memset(kv_mask[:], 0.0).then_inc(masks_zero, 1)
            dve.memset(head_ones[:], 0.0).then_inc(masks_zero, 1)
            dve.wait_ge(masks_zero, 2)
            mask = kv_mask[:].rearrange("p (w a b d) -> p w a b d", w=2, a=PAIRS, b=2)
            for b in range(2):
                rows = slice(b * KEYS, (b + 1) * KEYS)
                dve.memset(mask[rows, 0, :, b, :], SCALE).then_inc(masks_made, 1)
                dve.memset(mask[rows, 1, :, b, :], 1.0).then_inc(masks_made, 1)
                dve.memset(head_ones[rows, b * HD:(b + 1) * HD], 1.0).then_inc(masks_made, 1)

            def statistics(s, par):
                dve.wait_ge(x_loaded[par], (s - par) * 8 + 16)
                for t in range(T):
                    op = dve.bn_stats(stats[:, t], x_raw[:, par, t])
                op.then_inc(stats_part, 1)

            def mean_variance(s):
                for t in range(T):
                    op = dve.bn_aggr(mean_var[:, t], stats[:, t])
                op.then_inc(stats_ready, 1)

            def statistics_done(s):
                dve.wait_ge(stats_part, s + 1)
                dve.wait_ge(var_ready, past(s))

            def normalise(s, par):
                dve.wait_ge(stats_ready, s + 1)
                dve.wait_ge(rstd_ready, s + 1)
                dve.wait_ge(xt_psum, past(s * DH))
                for t in range(T):
                    op = dve.tensor_scalar(xn[:, t], x_raw[:, par, t], mean_var[:, t, 0:1], rstd[:, t:t + 1],
                                           ALU.subtract, ALU.mult)
                op.then_inc(xn_ready, 1)

            def shift_scores(s, n):
                pair = PAIR_ORDER[n]
                ps = s_bank[n % 2][:].rearrange("p (t n i) -> p t n i", t=T, n=NB)
                dve.wait_ge(s_psum, (s + 1) * PAIRS + n + 1)
                dve.tensor_reduce(s_max[:, pair], ps.rearrange("p t n i -> p n t i"), AX.XY,
                                  ALU.max).then_inc(max_ready, 1)
                if n == 0:
                    dve.wait_ge(pv_psum, past((s + 1) * QUADS))
                dve.wait_ge(max_ready, (s + 1) * PAIRS + n + 1)
                top = s_max[:, pair].unsqueeze(1).unsqueeze(3).to_broadcast([P, T, NB, PB])
                dve.tensor_tensor(w_exp[:, pair].rearrange("p (t n i) -> p t n i", t=T, n=NB), ps, top,
                                  ALU.subtract).then_inc(s_shifted, 1)

            def invert_den(s, part):
                quad, n = part // (RP // QUADS), part % (RP // QUADS)
                columns = slice(n * SEG * QUADS // RP, (n + 1) * SEG * QUADS // RP)
                dve.wait_ge(den_ready, s * QUADS + quad + 1)
                dve.reciprocal(den[:, quad, columns], den[:, quad, columns]).then_inc(rden_ready, 1)

            def transposed_lo(s, par):
                for c in range(DH):
                    dve.wait_ge(xt_hi, (s + 2) * DH + c + 1)
                    dve.wait_ge(xkey_hi, (s + 2) * DH + c + 1)
                    dve.tensor_tensor(xt[1][:, par, c], misc[c][:], f32(xt[0][:, par, c]),
                                      ALU.subtract).then_inc(xt_lo, 1)
                    dve.tensor_tensor(xkey[1][:, c].rearrange("p (a k) -> p a k", a=2),
                                      misc[c][:, 0:P:2].unsqueeze(1).to_broadcast([P, 2, KEYS]),
                                      f32(xkey[0][:, c]).rearrange("p (a k) -> p a k", a=2),
                                      ALU.subtract).then_inc(xkey_lo, 1)

            def project_in(s, par):
                if isinstance(s, int) and s == -2:
                    dve.wait_ge(masks_made, 6)
                dve.wait_ge(kv_psum, s + 3)
                dve.tensor_tensor(kv[:, par], misc[0][:], kv_mask[:], ALU.mult).then_inc(kv_ready, 1)
                for m in range(DH):
                    dve.wait_ge(q_hi, (s + 2) * DH + m + 1)
                    dve.tensor_tensor(q_part[1][:, m], h_bank[m][:], f32(q_part[0][:, m]),
                                      ALU.subtract).then_inc(q_lo, 1)
                dve.wait_ge(k_hi, s + 3)
                dve.tensor_tensor(k_part[1][:].rearrange("p c k -> p (c k)"), s_bank[0][:, 0:DH * P],
                                  f32(k_part[0][:]).rearrange("p c k -> p (c k)"), ALU.subtract).then_inc(k_lo, 1)

            def step(s, par, ffn, attention, norm, load):
                for n in range(PAIRS):
                    if n == 6 and norm:
                        transposed_lo(s, par)
                    if attention:
                        shift_scores(s, n)
                    if n == 1 and norm:
                        normalise(s + 2, par)
                        if isinstance(s, int) and s == -2:
                            for w in range(2):
                                split_lo(w)
                    if n in (2, 4) and ffn:
                        invert_den(s, RP // QUADS + n // 2 - 1)
                if isinstance(s, int) and s == -2:
                    split_lo(2)
                if norm:
                    project_in(s, par)
                if attention:
                    invert_den(s + 1, 0)
                if load:
                    statistics(s + 3, 1 - par)
                    statistics_done(s + 3)
                if isinstance(s, int) and s == -2:
                    for w in range(3, len(splits)):
                        split_lo(w)
                if attention:
                    invert_den(s + 1, 1)
                if load:
                    mean_variance(s + 3)
                if ffn:
                    dve.wait_ge(x_b2_ready, s + 1)
                    dve.wait_ge(y_stored[par], past((s - par) * 8))
                    for b in range(YB):
                        dve.wait_ge(y_psum, s * YB + b + 1)
                        dve.tensor_tensor(y[:, par, 2 * b:2 * b + 2],
                                          y_bank[b][:].rearrange("p (t d) -> p t d", t=2),
                                          x_b2[:, par, 2 * b:2 * b + 2], ALU.add).then_inc(y_ready, 1)

            statistics(0, 0)
            statistics_done(0)
            mean_variance(0)
            iterations(dve, step)

        @block.tensor
        def _(pe):
            def three_products(ps, pairs, start, stop, alone=True):
                for c, (stationary, moving) in enumerate(pairs):
                    for n, (a, b) in enumerate(((0, 0), (0, 1), (1, 0))):
                        mm = pe.matmul(ps, stationary[a], moving[b], start=start and c == 0 and n == 0,
                                       stop=stop and c == len(pairs) - 1 and n == 2, skip_group_check=not alone)
                return mm

            def first_product(s, i, par, attention=True):
                n = s * NH + i
                if isinstance(n, int) and n == 0:
                    pe.wait_ge(w_lo, 3)
                if isinstance(n, int) and n < 2:
                    pe.wait_ge(q_lo, i + 1)
                elif isinstance(n, int) and n in (EARLY, EARLY + 1):
                    pe.wait_ge(q_lo, 2 * DH)
                elif i < 2 and attention:
                    pe.wait_ge(q_lo, (s + 1) * DH + i + 1)
                elif i >= 2:
                    pe.wait_ge(h_ready, n - 1)
                three_products(h_bank[i % 2][:],
                               [([w[:, c, i * P:(i + 1) * P] for w in w1s], [x_[:, par, c] for x_ in xt])
                                for c in range(DH)], True, True).then_inc(h_psum, 1)

            def second_product(s, i):
                n = s * NH + i
                if isinstance(s, int) and s == 0 and i == 0:
                    pe.wait_ge(w_lo, len(splits))
                pe.wait_ge(h_hi, n + 1)
                pe.wait_ge(h_lo, n + 1)
                for t in range(T):
                    if i == 0 and t % 2 == 0:
                        pe.wait_ge(y_ready, past((s - 1) * YB + t // 2 + 1))
                    mm = three_products(y_bank[t // 2][:, (t % 2) * D:(t % 2 + 1) * D],
                                        [([h[:, i % HBUF, t * P:(t + 1) * P] for h in h_part],
                                          [w[:, i, :] for w in w2s])], i == 0 and t % 2 == 0, False, alone=False)
                mm.then_inc(h_used, 1)

            def output_product(s, par):
                pe.wait_ge(att_hi, (s + 1) * QUADS)
                pe.wait_ge(att_lo, (s + 1) * QUADS)
                for t in range(T):
                    mm = three_products(y_bank[t // 2][:, (t % 2) * D:(t % 2 + 1) * D],
                                        [([a[:, par, m, t * P:(t + 1) * P] for a in att_part],
                                          [w[:, m, :] for w in wout]) for m in range(DH)],
                                        False, t % 2 == 1, alone=False)
                    if t % 2 == 1:
                        mm.then_inc(y_psum, 1)

            def scores(s, n):
                pair = PAIR_ORDER[n]
                if n % 2 == 0:
                    pe.wait_ge(pair_packed[n // 2], (s + 2) * PACKED)
                pe.wait_ge(s_shifted, past((s + 1) * PAIRS + n - 1))
                pe.matmul(s_bank[n % 2][:], k_pack[0:PR, pair], q_pack[0:PR, pair], start=True,
                          stop=True).then_inc(s_psum, 1)

            def transpose_x(s, first):
                pe.wait_ge(xn_ready, s + 3)
                if isinstance(s, int) and s == -2:
                    pe.wait_ge(consts_made, 3)
                for c in range(DH):
                    pe.wait_ge((num_ready, den_ready)[c], past((s + 1) * QUADS))
                    if first:
                        pe.wait_ge((kv_ready, xt_lo)[c], past((s + 2) * (1, DH)[c]))
                    for t in range(T):
                        mm = pe.transpose(misc[c][:, t * P:(t + 1) * P], xn[:, t, c * P:(c + 1) * P], identity[:])
                    mm.then_inc(xt_psum, 1)

            def keys_values(s, par):
                if isinstance(s, int) and s == -2:
                    pe.wait_ge(w_lo, 2)
                for ready in (xt_hi, xt_lo, xkey_hi, xkey_lo):
                    pe.wait_ge(ready, (s + 3) * DH)
                three_products(misc[0][:], [([k[:, c] for k in xkey], [w[:, c] for w in wkv]) for c in range(DH)],
                               True, True).then_inc(kv_psum, 1)

            def transpose_k(s, par):
                pe.wait_ge(kv_ready, s + 3)
                pe.wait_ge(s_shifted, past((s + 2) * PAIRS))
                for m in range(DH):
                    mm = pe.transpose(s_bank[0][:, m * P:(m + 1) * P], kv[:, par, m * P:(m + 1) * P], identity[:])
                mm.then_inc(kt_psum, 1)

            def queries(s, par):
                for m in range(DH):
                    if isinstance(s, int) and s == -1:
                        pe.wait_ge(h_ready, EARLY)
                    else:
                        pe.wait_ge(h_ready, past(s * NH + NH - 1 + m))
                    three_products(h_bank[m][:], [([w[:, c, m * P:(m + 1) * P] for w in wq],
                                                   [x_[:, par, c] for x_ in xt]) for c in range(DH)],
                                   True, True).then_inc(q_psum, 1)

            def weighted_values(s, quad, par, norm):
                pe.wait_ge(w_ready, (s + 1) * PAIRS + PAIRS - (QUADS - 1 - quad))
                for b, (drained, stationary) in enumerate((
                        (num_ready, lambda p: kv[:, 1 - par, D + 32 * p:D + 32 * p + 32]),
                        (den_ready, lambda p: head_ones[:]))):
                    if quad == 0 and norm:
                        pe.wait_ge(kv_ready, s + 3)
                        pe.wait_ge(xt_lo, (s + 3) * DH)
                    else:
                        pe.wait_ge(drained, (s + 1) * QUADS + quad)
                    for j in range(PAIRS // QUADS):
                        pair = quad * (PAIRS // QUADS) + j
                        mm = pe.matmul(misc[b][32 * j:32 * j + 32, :], stationary(pair), w_exp[:, pair],
                                       start=True, stop=True)
                mm.then_inc(pv_psum, 1)

            def step(s, par, ffn, attention, norm, load):
                first, second = tile_steps(s, ffn)
                if attention:
                    scores(s, 0)
                    scores(s, 1)
                for i in range(LAG, NH):
                    if i == NH - 1 and norm:
                        transpose_x(s, not ffn)
                    if i in first:
                        first_product(past(s), first[i], par if ffn else 1 - par)
                    if attention and i > LAG:
                        scores(s, i - 1)
                    if i in second:
                        second_product(past(s), second[i])
                if ffn:
                    second_product(s, NH - 2)
                if attention:
                    scores(s, NH - 1)
                if norm:
                    keys_values(s, par)
                    queries(s, par)
                    transpose_k(s, par)
                if ffn:
                    second_product(s, NH - 1)
                if attention:
                    weighted_values(s, 0, par, norm)
                segment, tiles = tail_tiles(s, attention)
                for i in tiles:
                    first_product(segment, i, 1 - par if attention else par, norm)
                if attention:
                    weighted_values(s, 1, par, norm)
                if ffn:
                    output_product(s, par)

            iterations(pe, step)


def kernel(L0_attn_x, L0_attn_Wqkv, L0_attn_Wout, L0_ffn_W1, L0_ffn_b1, L0_ffn_W2, L0_ffn_b2):
    import numpy as np
    import concourse.bacc as bacc
    from concourse.bass_utils import run_bass_kernel_spmd

    wqkv = np.asarray(L0_attn_Wqkv)
    arrays = {
        "x": np.asarray(L0_attn_x),
        "wq_t": wqkv[:D].T,
        "wkv_t": wqkv[D:].T,
        "wout_t": np.asarray(L0_attn_Wout).T,
        "w1": np.asarray(L0_ffn_W1),
        "b1": np.asarray(L0_ffn_b1).reshape(-1, P).T,
        "w2": np.asarray(L0_ffn_W2),
        "b2": np.asarray(L0_ffn_b2),
    }
    arrays = {name: np.ascontiguousarray(a) for name, a in arrays.items()}
    nc = bacc.Bacc("TRN2", target_bir_lowering=False, num_devices=1)
    args = [nc.dram_tensor(name, a.shape, mybir.dt.from_np(a.dtype), kind="ExternalInput").ap()
            for name, a in arrays.items()]
    out = nc.dram_tensor("out", arrays["x"].shape, F32, kind="ExternalOutput").ap()
    ln_attention_ffn(nc, *args, out)
    r = run_bass_kernel_spmd(nc, [arrays], core_ids=[0])
    return r.results[0]["out"]
```

```python
from contextlib import ExitStack

import concourse.bass as bass
from concourse import mybir

F32 = mybir.dt.float32
F32R = mybir.dt.float32r
ALU = mybir.AluOpType
ACT = mybir.ActivationFunctionType
AX = mybir.AxisListType

P = 128
H = 16
HD = 16
SEG = 512
DIL = 8
BLOCK_M = 64
KEYS = SEG // DIL
T = SEG // P
NB = SEG // BLOCK_M
PB = P // NB
PAIRS = H // 2
PW = 2 * HD
PR = 3 * PW
QUADS = 2
D = H * HD
DH = D // P
EPS = 1e-5
GUARD = 1e-10


def ln_attention_ffn(nc, x, wq_t, wkv_t, wout_t, w1, b1, w2, b2, out):
    NSEG = x.shape[0] * x.shape[1] // SEG
    INTER = w1.shape[1]
    NH = INTER // P
    SCALE = float(HD) ** -0.5
    HBUF = 4
    LAG = 2
    EARLY = 5
    RP = 4
    YB = 2
    PAIR_ORDER = [half * (PAIRS // 2) + j for j in range(PAIRS // 2) for half in range(DH)]
    PACKED = 16 * 6
    assert D == 256 and x.shape[2] == D and NSEG % 2 == 0 and NH == PAIRS and 2 * KEYS == P
    assert T == 4 and PB * NB == P

    x_rows = x.rearrange("b (s p t) d -> (b s) p t d", p=P, t=T)
    x_key_rows = x.rearrange("b (k i) d -> (b k) i d", i=DIL)[:, 0]
    out_rows = out.rearrange("b (s p t) d -> (b s) p t d", p=P, t=T)

    with ExitStack() as ctx:
        def sb(name, shape, dt):
            return ctx.enter_context(nc.sbuf_tensor(name, shape, dt))

        def sem(name):
            return ctx.enter_context(nc.semaphore(name))

        identity = sb("identity", [P, P], F32)
        k_mask_t = sb("k_mask_t", [P, P], F32)
        k_mask = sb("k_mask", [P, P], F32)
        head_ones = sb("head_ones", [P, PW], F32)
        minus_half = sb("minus_half", [P, T + 1], F32)
        eps = sb("eps", [P, T + 1], F32)
        b1_cols = sb("b1_cols", [P, NH], F32)
        b2_rows = sb("b2_rows", [P, D], F32)
        wq = [sb(f"wq_{n}", [P, DH, D], F32R) for n in ("hi", "lo")]
        wkv = [sb(f"wkv_{n}", [P, DH, 2 * D], F32R) for n in ("hi", "lo")]
        wout = [sb(f"wout_{n}", [P, DH, D], F32R) for n in ("hi", "lo")]
        w1s = [sb(f"w1_{n}", [P, DH, INTER], F32R) for n in ("hi", "lo")]
        w2s = [sb(f"w2_{n}", [P, NH, D], F32R) for n in ("hi", "lo")]
        x_raw = sb("x_raw", [P, 2, T, D], F32)
        x_keys = sb("x_keys", [P, D], F32)
        x_b2 = sb("x_b2", [P, 2, T, D], F32)
        stats = sb("stats", [P, T + 1, 6], F32)
        mean_var = sb("mean_var", [P, T + 1, 2], F32)
        var_eps = sb("var_eps", [P, T + 1], F32)
        rstd = sb("rstd", [P, T + 1], F32)
        xn = sb("xn", [P, T, D], F32)
        xn_keys = sb("xn_keys", [P, D], F32)
        xt = [sb(f"xt_{n}", [P, 2, DH, SEG], F32R) for n in ("hi", "lo")]
        xkey = [sb(f"xkey_{n}", [P, DH, P], F32R) for n in ("hi", "lo")]
        q_part = [sb(f"q_{n}", [P, DH, SEG], F32R) for n in ("hi", "lo")]
        q_pack = sb("q_pack", [P, PAIRS, SEG], F32R)
        kv = sb("kv", [P, 2 * D], F32)
        v = sb("v", [P, 2, D], F32)
        k_full = sb("k_full", [P, 2, DH, P], F32)
        k_part = [sb(f"k_{n}", [P, DH, P], F32R) for n in ("hi", "lo")]
        k_pack = sb("k_pack", [P, PAIRS, P], F32R)
        s_max = sb("s_max", [P, PAIRS, NB], F32)
        w_exp = sb("w_exp", [P, PAIRS, SEG], F32)
        num = sb("num", [P, QUADS, SEG], F32)
        den = sb("den", [P, QUADS, SEG], F32)
        att = sb("att", [P, QUADS, SEG], F32)
        att_part = [sb(f"att_{n}", [P, 2, QUADS, SEG], F32R) for n in ("hi", "lo")]
        h_full = sb("h_full", [P, HBUF, SEG], F32)
        h_part = [sb(f"h_{n}", [P, HBUF, SEG], F32R) for n in ("hi", "lo")]
        y = sb("y", [P, 2, T, D], F32)
        w1_raw = w_exp[:].rearrange("p a b -> p (a b)")[:, 0:DH * INTER].rearrange("p (c n) -> p c n", c=DH)
        w2_raw = w_exp[:].rearrange("p a b -> p (a b)")[:, DH * INTER:].rearrange("p (c n) -> p c n", c=NH)
        wkv_raw = y[:].rearrange("p a b c -> p (a b c)")[:, 0:2 * DH * D].rearrange("p (c n) -> p c n", c=DH)
        wq_raw = y[:].rearrange("p a b c -> p (a b c)")[:, 2 * DH * D:3 * DH * D].rearrange("p (c n) -> p c n", c=DH)
        wout_raw = y[:].rearrange("p a b c -> p (a b c)")[:, 3 * DH * D:].rearrange("p (c n) -> p c n", c=DH)

        def bank(name):
            return ctx.enter_context(nc.psum_tensor(name, [P, SEG], F32))
        misc = [bank(f"misc{i}") for i in range(2)]
        h_bank = [bank(f"h_bank{i}") for i in range(2)]
        s_bank = [bank(f"s_bank{i}") for i in range(2)]
        y_bank = [bank(f"y_bank{i}") for i in range(YB)]

        def key_banks(s):
            return (s_bank[0], s_bank[1]) if isinstance(s, int) and s == -2 else (misc[1], misc[0])

        const_loaded = sem("const_loaded")
        wqkv_loaded = sem("wqkv_loaded")
        w1_loaded = sem("w1_loaded")
        w2_loaded = sem("w2_loaded")
        identity_zero = sem("identity_zero")
        consts_made = sem("consts_made")
        masks_zero = sem("masks_zero")
        masks_made = sem("masks_made")
        k_mask_psum = sem("k_mask_psum")
        w_hi = sem("w_hi")
        w_lo = sem("w_lo")
        x_loaded = [sem(f"x_loaded{i}") for i in range(2)]
        x_keys_loaded = sem("x_keys_loaded")
        x_b2_ready = sem("x_b2_ready")
        stats_part = sem("stats_part")
        stats_ready = sem("stats_ready")
        var_ready = sem("var_ready")
        rstd_ready = sem("rstd_ready")
        xn_ready = sem("xn_ready")
        xn_keys_ready = sem("xn_keys_ready")
        xkey_psum = sem("xkey_psum")
        xkey_hi = sem("xkey_hi")
        xkey_lo = sem("xkey_lo")
        kv_psum = sem("kv_psum")
        kv_ready = sem("kv_ready")
        kt_psum = sem("kt_psum")
        k_ready = sem("k_ready")
        xt_psum = sem("xt_psum")
        xt_hi = sem("xt_hi")
        xt_lo = sem("xt_lo")
        q_psum = sem("q_psum")
        q_hi = sem("q_hi")
        q_lo = sem("q_lo")
        pair_packed = [sem(f"pair_packed{j}") for j in range(PAIRS // 2)]
        v_ready = sem("v_ready")
        k_hi = sem("k_hi")
        k_lo = sem("k_lo")
        s_psum = sem("s_psum")
        max_ready = sem("max_ready")
        s_shifted = sem("s_shifted")
        w_ready = sem("w_ready")
        pv_psum = sem("pv_psum")
        num_ready = sem("num_ready")
        den_ready = sem("den_ready")
        rden_ready = sem("rden_ready")
        att_ready = sem("att_ready")
        att_hi = sem("att_hi")
        att_lo = sem("att_lo")
        h_psum = sem("h_psum")
        h_ready = sem("h_ready")
        h_hi = sem("h_hi")
        h_lo = sem("h_lo")
        h_used = sem("h_used")
        y_psum = sem("y_psum")
        y_ready = sem("y_ready")
        y_stored = [sem(f"y_stored{i}") for i in range(2)]

        def past(count):
            return max(count, 0) if isinstance(count, int) else count

        def iterations(eng, first_step, step):
            def fixed(s):
                step(s, s % 2, s >= 0, 0 <= s + 1 < NSEG, s + 2 < NSEG, s + 3 < NSEG)

            first_step()
            for s in range(-1, 2):
                fixed(s)
            with eng.Fori(1, NSEG // 2 - 2) as half:
                step(half * 2, 0, True, True, True, True)
                step(half * 2 + 1, 1, True, True, True, True)
            for s in range(NSEG - 4, NSEG):
                fixed(s)

        def tiles(par):
            return T + 1 - par

        def tile_steps(s, ffn):
            if isinstance(s, int) and s == -1:
                return {i: i for i in range(LAG, EARLY)}, {i: i - LAG for i in range(LAG, EARLY)}
            if isinstance(s, int) and s == 0:
                return {LAG + 2 + i: EARLY + LAG + i for i in range(NH - EARLY - LAG)}, \
                       {LAG + 2 + i: EARLY - LAG + i for i in range(NH - EARLY)}
            if not ffn:
                return {}, {}
            return {i: i for i in range(LAG, NH)}, {i: i - LAG for i in range(LAG, NH)}

        def tail_tiles(s, attention):
            if isinstance(s, int) and s < 0:
                return 0, [(0, 1), (EARLY, EARLY + 1)][s + 2]
            return s + 1, (0, 1) if attention else ()

        splits = [(wkv_raw, wkv, wqkv_loaded, 32), (wq_raw, wq, wqkv_loaded, 32), (w1_raw, w1s, w1_loaded, 16),
                  (w2_raw, w2s, w2_loaded, 32), (wout_raw, wout, w2_loaded, 32)]

        def f32(tile):
            return tile.bitcast(F32)

        block = ctx.enter_context(nc.Block())

        @block.sync
        def _(sp):
            def load_x(seg, par):
                sp.dma_start(x_raw[:, par], x_rows[seg]).then_inc(x_loaded[par], 16)

            def load_keys(seg):
                sp.dma_start(x_keys[:], x_key_rows[bass.ds(seg * KEYS, P)]).then_inc(x_keys_loaded, 16)

            def first_step():
                load_keys(0)
                load_x(0, 0)
                sp.dma_start(wq_raw, wq_t.rearrange("(c p) n -> p c n", p=P)).then_inc(wqkv_loaded, 16)
                sp.dma_start(wkv_raw, wkv_t.rearrange("(c p) n -> p c n", p=P)).then_inc(wqkv_loaded, 16)
                sp.dma_start(w1_raw, w1.rearrange("(c p) n -> p c n", p=P)).then_inc(w1_loaded, 16)
                sp.dma_start(w2_raw, w2.rearrange("(c p) n -> p c n", p=P)).then_inc(w2_loaded, 16)
                sp.dma_start(wout_raw, wout_t.rearrange("(c p) n -> p c n", p=P)).then_inc(w2_loaded, 16)
                sp.dma_start(b1_cols[:], b1).then_inc(const_loaded, 16)
                sp.dma_start(b2_rows[:], b2.partition_broadcast(P)).then_inc(const_loaded, 16)
                load_x(1, 1)
                pack(-2)

            def pack(s):
                for j in range(PAIRS // 2):
                    if j == 0:
                        sp.wait_ge(k_hi, s + 3)
                        sp.wait_ge(k_lo, s + 3)
                    for r, part in enumerate((0, 0, 1)):
                        sp.dma_start(f32(k_pack[PW * r:PW * (r + 1), j::PAIRS // 2, :]),
                                     f32(k_part[part][PW * j:PW * (j + 1)])).then_inc(pair_packed[j], 16)
                    if j == 0:
                        sp.wait_ge(q_hi, (s + 3) * DH)
                        sp.wait_ge(q_lo, (s + 3) * DH)
                    for r, part in enumerate((0, 1, 0)):
                        sp.dma_start(f32(q_pack[PW * r:PW * (r + 1), j::PAIRS // 2, :]),
                                     f32(q_part[part][PW * j:PW * (j + 1)])).then_inc(pair_packed[j], 16)

            def step(s, par, ffn, attention, norm, load):
                if load:
                    sp.wait_ge(x_b2_ready, s + 2)
                    sp.wait_ge(xn_ready, s + 2)
                    load_x(s + 3, 1 - par)
                if load and par == 1:
                    sp.wait_ge(xn_keys_ready, s + 3)
                    load_keys(s + 3)
                if norm:
                    pack(s)
                if ffn:
                    sp.wait_ge(y_ready, (s + 1) * YB)
                    sp.dma_start(out_rows[s], y[:, par]).then_inc(y_stored[par], 16)

            iterations(sp, first_step, step)
            for par in range(2):
                sp.wait_ge(y_stored[par], 16 * (NSEG // 2))

        @block.gpsimd
        def _(pool):
            pool.memset(minus_half[:], -0.5).then_inc(consts_made, 1)
            pool.memset(eps[:], EPS).then_inc(consts_made, 1)
            pool.memset(identity[:], 0.0).then_inc(identity_zero, 1)
            pool.wait_ge(identity_zero, 1)
            pool.affine_select(out=identity[:], in_=identity[:], compare_op=ALU.not_equal, fill=1.0,
                               base=0, pattern=[[-1, P]], channel_multiplier=1).then_inc(consts_made, 1)

            def inverse_deviation(s, par):
                pool.wait_ge(stats_ready, s + 1)
                pool.wait_ge(xn_ready, past(s))
                pool.wait_ge(consts_made, 3)
                w = tiles(par)
                pool.tensor_tensor(var_eps[:, 0:w], mean_var[:, 0:w, 1], eps[:, 0:w], ALU.add).then_inc(var_ready, 1)
                pool.wait_ge(var_ready, s + 1)
                pool.tensor_tensor(rstd[:, 0:w], var_eps[:, 0:w], minus_half[:, 0:w],
                                   ALU.pow).then_inc(rstd_ready, 1)

            def hidden_lo(s, i):
                n = s * NH + i
                pool.wait_ge(h_ready, n + 1)
                pool.wait_ge(h_hi, n + 1)
                pool.wait_ge(h_used, past(n - HBUF + 1))
                pool.tensor_tensor(h_part[1][:, i % HBUF], h_full[:, i % HBUF], f32(h_part[0][:, i % HBUF]),
                                   ALU.subtract).then_inc(h_lo, 1)

            def attention_out(s, quad):
                pool.wait_ge(rden_ready, (s * QUADS + quad + 1) * (RP // QUADS))
                pool.wait_ge(num_ready, s * QUADS + quad + 1)
                pool.wait_ge(att_hi, past((s - 1) * QUADS + quad + 1))
                pool.tensor_tensor(att[:, quad], num[:, quad], den[:, quad], ALU.mult).then_inc(att_ready, 1)

            def attention_lo(s, quad, par):
                pool.wait_ge(att_ready, s * QUADS + quad + 1)
                pool.wait_ge(att_hi, s * QUADS + quad + 1)
                pool.tensor_tensor(att_part[1][:, par, quad], att[:, quad], f32(att_part[0][:, par, quad]),
                                   ALU.subtract).then_inc(att_lo, 1)

            def residual(s, par):
                if isinstance(s, int) and s == -1:
                    pool.wait_ge(const_loaded, 32)
                pool.wait_ge(x_loaded[1 - par], (s + par) * 8 + 16)
                pool.wait_ge(y_ready, past(s * YB))
                pool.tensor_tensor(x_b2[:, 1 - par], x_raw[:, 1 - par],
                                   b2_rows[:].unsqueeze(1).to_broadcast([P, T, D]), ALU.add).then_inc(x_b2_ready, 1)

            def step(s, par, ffn, attention, norm, load):
                first, _ = tile_steps(s, ffn)
                for i in range(LAG, NH):
                    if i in first:
                        hidden_lo(past(s), first[i])
                    if i == 2 and attention:
                        residual(s, par)
                    if i in (4, 6) and ffn:
                        attention_out(s, i // 2 - 2)
                    if i in (5, 7) and ffn:
                        attention_lo(s, i // 2 - 2, par)
                segment, tail = tail_tiles(s, attention)
                for i in tail:
                    hidden_lo(segment, i)
                if load:
                    inverse_deviation(s + 3, 1 - par)

            def first_step():
                inverse_deviation(0, 0)
                for i in range(LAG):
                    hidden_lo(0, i)
                inverse_deviation(1, 1)

            iterations(pool, first_step, step)

        @block.scalar
        def _(act):
            def split_hi(n):
                raw, parts, loaded, count = splits[n]
                act.wait_ge(loaded, count)
                act.copy(parts[0][:], raw).then_inc(w_hi, 1)

            def hidden(s, i):
                n = s * NH + i
                if isinstance(n, int) and n == 0:
                    act.wait_ge(const_loaded, 32)
                act.wait_ge(h_psum, n + 1)
                act.wait_ge(h_lo, past(n - HBUF + 1))
                act.wait_ge(h_used, past(n - HBUF + 1))
                act.activation(h_part[0][:, i % HBUF], h_bank[i % 2][:], ACT.Relu,
                               bias=b1_cols[:, i:i + 1]).then_inc(h_hi, 1)
                act.activation(h_full[:, i % HBUF], h_bank[i % 2][:], ACT.Relu,
                               bias=b1_cols[:, i:i + 1]).then_inc(h_ready, 1)

            def exponential(s, n):
                pair = PAIR_ORDER[n]
                act.wait_ge(s_shifted, (s + 1) * PAIRS + n + 1)
                act.activation(w_exp[:, pair], w_exp[:, pair], ACT.Exp).then_inc(w_ready, 1)

            def attention_hi(s, quad, par):
                act.wait_ge(att_ready, s * QUADS + quad + 1)
                act.wait_ge(y_psum, past((s - 1) * YB))
                act.copy(att_part[0][:, par, quad], att[:, quad]).then_inc(att_hi, 1)

            def attention_drain(s, quad):
                n = (s + 1) * QUADS + quad + 1
                act.wait_ge(pv_psum, n)
                act.wait_ge(att_ready, past(n - QUADS))
                act.copy(num[:, quad], misc[0][:]).then_inc(num_ready, 1)
                act.add(den[:, quad], misc[1][:], GUARD).then_inc(den_ready, 1)

            def keys_hi(s):
                act.wait_ge(xkey_psum, s + 4)
                act.wait_ge(kv_psum, past(s + 2))
                act.copy(xkey[0][:].rearrange("p c k -> p (c k)"),
                         key_banks(s)[0][:, 0:DH * P]).then_inc(xkey_hi, 2)

            def transposed_hi(s, par):
                act.wait_ge(h_psum, past((s + 1) * NH))
                for c in range(DH):
                    act.wait_ge(xt_psum, (s + 2) * DH + c + 1)
                    act.copy(xt[0][:, par, c], misc[c][:]).then_inc(xt_hi, 1)

            def queries_hi(s, m):
                act.wait_ge(q_psum, (s + 2) * DH + m + 1)
                act.copy(q_part[0][:, m], h_bank[m][:]).then_inc(q_hi, 1)

            def pair_keys_hi(s, par):
                act.wait_ge(k_ready, s + 3)
                act.copy(k_part[0][:], k_full[:, par]).then_inc(k_hi, 1)

            def first_step():
                for n in range(2):
                    split_hi(n)
                keys_hi(-2)
                transposed_hi(-2, 0)
                split_hi(2)
                queries_hi(-2, 0)
                pair_keys_hi(-2, 0)
                queries_hi(-2, 1)
                for n in range(3, len(splits)):
                    split_hi(n)
                for i in range(LAG):
                    hidden(0, i)

            def step(s, par, ffn, attention, norm, load):
                first, _ = tile_steps(s, ffn)
                for i in range(LAG, NH - 1):
                    if i == 3 and norm and par == 0:
                        keys_hi(s)
                    if attention:
                        exponential(s, i - LAG)
                    if i in first:
                        hidden(past(s), first[i])
                    if i == 5 and ffn:
                        attention_hi(s, 0, par)
                if norm:
                    transposed_hi(s, par)
                if NH - 1 in first:
                    hidden(s, NH - 1)
                if attention:
                    exponential(s, PAIRS - 3)
                if ffn:
                    attention_hi(s, 1, par)
                if attention:
                    exponential(s, PAIRS - 2)
                if norm:
                    pair_keys_hi(s, par)
                if attention:
                    exponential(s, PAIRS - 1)
                if norm:
                    for m in range(DH):
                        queries_hi(s, m)
                if attention:
                    attention_drain(s, 0)
                segment, tail = tail_tiles(s, attention)
                for i in tail:
                    hidden(segment, i)
                if attention:
                    attention_drain(s, 1)

            iterations(act, first_step, step)

        @block.vector
        def _(dve):
            def split_lo(n):
                raw, parts, loaded, count = splits[n]
                dve.wait_ge(loaded, count)
                dve.wait_ge(w_hi, n + 1)
                dve.tensor_tensor(parts[1][:], raw, f32(parts[0][:]), ALU.subtract).then_inc(w_lo, 1)

            dve.memset(k_mask_t[:], 0.0).then_inc(masks_zero, 1)
            dve.memset(head_ones[:], 0.0).then_inc(masks_zero, 1)
            dve.memset(v[:].rearrange("p s d -> p (s d)"), 0.0).then_inc(masks_zero, 1)
            dve.wait_ge(masks_zero, 3)
            for b in range(2):
                rows = slice(b * KEYS, (b + 1) * KEYS)
                dve.memset(k_mask_t[rows].rearrange("p (a b d) -> p a b d", b=2, d=HD)[:, :, b, :],
                           SCALE).then_inc(masks_made, 1)
                dve.memset(head_ones[rows, b * HD:(b + 1) * HD], 1.0).then_inc(masks_made, 1)
            dve.wait_ge(k_mask_psum, 1)
            dve.tensor_copy(k_mask[:], s_bank[1][:, 0:P]).then_inc(masks_made, 1)

            def statistics(s, par):
                dve.wait_ge(x_loaded[par], (s - par) * 8 + 16)
                for t in range(T):
                    op = dve.bn_stats(stats[:, t], x_raw[:, par, t])
                if par == 0:
                    dve.wait_ge(x_keys_loaded, s * 8 + 16)
                    op = dve.bn_stats(stats[:, T], x_keys[:])
                op.then_inc(stats_part, 1)

            def mean_variance(s, par):
                for t in range(tiles(par)):
                    op = dve.bn_aggr(mean_var[:, t], stats[:, t])
                op.then_inc(stats_ready, 1)

            def statistics_done(s):
                dve.wait_ge(stats_part, s + 1)
                dve.wait_ge(var_ready, past(s))

            def normalise_keys(s):
                dve.wait_ge(stats_ready, s + 1)
                dve.wait_ge(rstd_ready, s + 1)
                dve.wait_ge(xkey_psum, past(s))
                dve.tensor_scalar(xn_keys[:], x_keys[:], mean_var[:, T, 0:1], rstd[:, T:T + 1],
                                  ALU.subtract, ALU.mult).then_inc(xn_keys_ready, 2)

            def keys_lo(s):
                dve.wait_ge(xkey_hi, s + 4)
                dve.tensor_tensor(xkey[1][:].rearrange("p c k -> p (c k)"), key_banks(s)[0][:, 0:DH * P],
                                  f32(xkey[0][:]).rearrange("p c k -> p (c k)"),
                                  ALU.subtract).then_inc(xkey_lo, 2)

            def drain_kv(s):
                dve.wait_ge(kv_psum, s + 4)
                dve.tensor_copy(kv[:], key_banks(s)[1][:]).then_inc(kv_ready, 2)

            def mask_k(s):
                dve.wait_ge(kt_psum, s + 4)
                kt = key_banks(s)[0][:, 0:DH * P].rearrange("p (c s k) -> p c s k", c=DH, s=2)
                for seg in range(2):
                    dve.tensor_tensor(k_full[:, seg].rearrange("p c (a k) -> p c a k", a=2),
                                      kt[:, :, seg].unsqueeze(2).to_broadcast([P, DH, 2, KEYS]),
                                      k_mask[:].rearrange("p (a k) -> p a k", a=2).unsqueeze(1).to_broadcast(
                                          [P, DH, 2, KEYS]), ALU.mult).then_inc(k_ready, 1)

            def normalise(s, par):
                dve.wait_ge(stats_ready, s + 1)
                dve.wait_ge(rstd_ready, s + 1)
                dve.wait_ge(xt_psum, past(s * DH))
                for t in range(T):
                    op = dve.tensor_scalar(xn[:, t], x_raw[:, par, t], mean_var[:, t, 0:1], rstd[:, t:t + 1],
                                           ALU.subtract, ALU.mult)
                op.then_inc(xn_ready, 1)

            def shift_scores(s, n):
                pair = PAIR_ORDER[n]
                ps = s_bank[n % 2][:].rearrange("p (t n i) -> p t n i", t=T, n=NB)
                dve.wait_ge(s_psum, (s + 1) * PAIRS + n + 1)
                dve.tensor_reduce(s_max[:, pair], ps.rearrange("p t n i -> p n t i"), AX.XY,
                                  ALU.max).then_inc(max_ready, 1)
                if n == 0:
                    dve.wait_ge(pv_psum, past((s + 1) * QUADS))
                dve.wait_ge(max_ready, (s + 1) * PAIRS + n + 1)
                top = s_max[:, pair].unsqueeze(1).unsqueeze(3).to_broadcast([P, T, NB, PB])
                dve.tensor_tensor(w_exp[:, pair].rearrange("p (t n i) -> p t n i", t=T, n=NB), ps, top,
                                  ALU.subtract).then_inc(s_shifted, 1)

            def invert_den(s, part):
                quad, n = part // (RP // QUADS), part % (RP // QUADS)
                columns = slice(n * SEG * QUADS // RP, (n + 1) * SEG * QUADS // RP)
                dve.wait_ge(den_ready, s * QUADS + quad + 1)
                dve.reciprocal(den[:, quad, columns], den[:, quad, columns]).then_inc(rden_ready, 1)

            def transposed_lo(s, par):
                for c in range(DH):
                    dve.wait_ge(xt_hi, (s + 2) * DH + c + 1)
                    dve.tensor_tensor(xt[1][:, par, c], misc[c][:], f32(xt[0][:, par, c]),
                                      ALU.subtract).then_inc(xt_lo, 1)

            def finish_projections(s, par):
                dve.wait_ge(k_hi, s + 3)
                dve.tensor_tensor(k_part[1][:], k_full[:, par], f32(k_part[0][:]), ALU.subtract).then_inc(k_lo, 1)
                for m in range(DH):
                    dve.wait_ge(q_hi, (s + 2) * DH + m + 1)
                    dve.tensor_tensor(q_part[1][:, m], h_bank[m][:], f32(q_part[0][:, m]),
                                      ALU.subtract).then_inc(q_lo, 1)
                dve.wait_ge(kv_ready, s + 3)
                dve.wait_ge(pv_psum, past((s + 1) * QUADS))
                for a in range(2):
                    dve.tensor_copy(
                        v[a * KEYS:(a + 1) * KEYS, par].rearrange("p (n a d) -> p n a d", a=2, d=HD)[:, :, a, :],
                        kv[par * KEYS:(par + 1) * KEYS, D:].rearrange("p (n a d) -> p n a d", a=2, d=HD)[:, :, a, :]
                    ).then_inc(v_ready, 1)

            def step(s, par, ffn, attention, norm, load):
                keys = norm and par == 0
                for n in range(PAIRS):
                    if n == 0 and keys:
                        normalise_keys(s + 2)
                    if n == 4 and keys:
                        drain_kv(s)
                    if n == 5 and keys:
                        mask_k(s)
                    if n == 6 and norm:
                        transposed_lo(s, par)
                    if attention:
                        shift_scores(s, n)
                    if n == 1 and norm:
                        normalise(s + 2, par)
                    if n == 1 and keys:
                        keys_lo(s)
                    if n in (2, 4) and ffn:
                        invert_den(s, RP // QUADS + n // 2 - 1)
                if norm:
                    finish_projections(s, par)
                if load:
                    statistics(s + 3, 1 - par)
                    statistics_done(s + 3)
                if attention:
                    invert_den(s + 1, 0)
                if load:
                    mean_variance(s + 3, 1 - par)
                if attention:
                    invert_den(s + 1, 1)
                if ffn:
                    dve.wait_ge(x_b2_ready, s + 1)
                    dve.wait_ge(y_stored[par], past((s - par) * 8))
                    for b in range(YB):
                        dve.wait_ge(y_psum, s * YB + b + 1)
                        dve.tensor_tensor(y[:, par, 2 * b:2 * b + 2],
                                          y_bank[b][:].rearrange("p (t d) -> p t d", t=2),
                                          x_b2[:, par, 2 * b:2 * b + 2], ALU.add).then_inc(y_ready, 1)

            def first_step():
                statistics(0, 0)
                statistics_done(0)
                mean_variance(0, 0)
                normalise_keys(0)
                normalise(0, 0)
                split_lo(0)
                split_lo(1)
                keys_lo(-2)
                transposed_lo(-2, 0)
                drain_kv(-2)
                split_lo(2)
                mask_k(-2)
                finish_projections(-2, 0)
                statistics(1, 1)
                statistics_done(1)
                for w in range(3, len(splits)):
                    split_lo(w)
                mean_variance(1, 1)

            iterations(dve, first_step, step)

        @block.tensor
        def _(pe):
            def three_products(ps, pairs, start, stop, alone=True):
                for c, (stationary, moving) in enumerate(pairs):
                    for n, (a, b) in enumerate(((0, 0), (0, 1), (1, 0))):
                        mm = pe.matmul(ps, stationary[a], moving[b], start=start and c == 0 and n == 0,
                                       stop=stop and c == len(pairs) - 1 and n == 2, skip_group_check=not alone)
                return mm

            def first_product(s, i, par, attention=True):
                n = s * NH + i
                if isinstance(n, int) and n == 0:
                    pe.wait_ge(w_lo, 3)
                if isinstance(n, int) and n < 2:
                    pe.wait_ge(q_lo, i + 1)
                elif isinstance(n, int) and n in (EARLY, EARLY + 1):
                    pe.wait_ge(q_lo, 2 * DH)
                elif i < 2 and attention:
                    pe.wait_ge(q_lo, (s + 1) * DH + i + 1)
                elif i >= 2:
                    pe.wait_ge(h_ready, n - 1)
                three_products(h_bank[i % 2][:],
                               [([w[:, c, i * P:(i + 1) * P] for w in w1s], [x_[:, par, c] for x_ in xt])
                                for c in range(DH)], True, True).then_inc(h_psum, 1)

            def second_product(s, i):
                n = s * NH + i
                if isinstance(s, int) and s == 0 and i == 0:
                    pe.wait_ge(w_lo, len(splits))
                pe.wait_ge(h_hi, n + 1)
                pe.wait_ge(h_lo, n + 1)
                for t in range(T):
                    if i == 0 and t % 2 == 0:
                        pe.wait_ge(y_ready, past((s - 1) * YB + t // 2 + 1))
                    mm = three_products(y_bank[t // 2][:, (t % 2) * D:(t % 2 + 1) * D],
                                        [([h[:, i % HBUF, t * P:(t + 1) * P] for h in h_part],
                                          [w[:, i, :] for w in w2s])], i == 0 and t % 2 == 0, False, alone=False)
                mm.then_inc(h_used, 1)

            def output_product(s, par):
                pe.wait_ge(att_hi, (s + 1) * QUADS)
                pe.wait_ge(att_lo, (s + 1) * QUADS)
                for t in range(T):
                    mm = three_products(y_bank[t // 2][:, (t % 2) * D:(t % 2 + 1) * D],
                                        [([a[:, par, m, t * P:(t + 1) * P] for a in att_part],
                                          [w[:, m, :] for w in wout]) for m in range(DH)],
                                        False, t % 2 == 1, alone=False)
                    if t % 2 == 1:
                        mm.then_inc(y_psum, 1)

            def scores(s, n):
                pair = PAIR_ORDER[n]
                if n % 2 == 0:
                    pe.wait_ge(pair_packed[n // 2], (s + 2) * PACKED)
                pe.wait_ge(s_shifted, past((s + 1) * PAIRS + n - 1))
                pe.matmul(s_bank[n % 2][:], k_pack[0:PR, pair], q_pack[0:PR, pair], start=True,
                          stop=True).then_inc(s_psum, 1)

            def transpose_x(s, par):
                pe.wait_ge(xn_ready, s + 3)
                pe.wait_ge(num_ready, past((s + 1) * QUADS))
                pe.wait_ge(den_ready, past((s + 1) * QUADS))
                if par == 0 and not (isinstance(s, int) and s == -2):
                    pe.wait_ge(kv_ready, s + 4)
                    pe.wait_ge(k_ready, s + 4)
                for c in range(DH):
                    for t in range(T):
                        mm = pe.transpose(misc[c][:, t * P:(t + 1) * P], xn[:, t, c * P:(c + 1) * P], identity[:])
                    mm.then_inc(xt_psum, 1)

            def transpose_keys(s):
                pe.wait_ge(xn_keys_ready, s + 4)
                pe.wait_ge(den_ready, past((s + 1) * QUADS))
                for c in range(DH):
                    mm = pe.transpose(key_banks(s)[0][:, c * P:(c + 1) * P], xn_keys[:, c * P:(c + 1) * P], identity[:])
                mm.then_inc(xkey_psum, 2)

            def keys_values(s):
                if isinstance(s, int) and s == -2:
                    pe.wait_ge(w_lo, 1)
                pe.wait_ge(xkey_hi, s + 4)
                pe.wait_ge(xkey_lo, s + 4)
                pe.wait_ge(num_ready, past((s + 1) * QUADS))
                three_products(key_banks(s)[1][:],
                               [([k[:, c] for k in xkey], [w[:, c] for w in wkv]) for c in range(DH)],
                               True, True).then_inc(kv_psum, 2)

            def transpose_k(s):
                pe.wait_ge(kv_ready, s + 4)
                for m in range(DH):
                    mm = pe.transpose(key_banks(s)[0][:, m * P:(m + 1) * P], kv[:, m * P:(m + 1) * P], identity[:])
                mm.then_inc(kt_psum, 2)

            def queries(s, par, m):
                if isinstance(s, int) and s == -2:
                    pe.wait_ge(w_lo, 2)
                pe.wait_ge(xt_hi, (s + 3) * DH)
                pe.wait_ge(xt_lo, (s + 3) * DH)
                if isinstance(s, int) and s == -1:
                    pe.wait_ge(h_ready, EARLY)
                else:
                    pe.wait_ge(h_ready, past(s * NH + NH - 1 + m))
                three_products(h_bank[m][:], [([w[:, c, m * P:(m + 1) * P] for w in wq],
                                               [x_[:, par, c] for x_ in xt]) for c in range(DH)],
                               True, True).then_inc(q_psum, 1)

            def weighted_values(s, quad, par, norm):
                pe.wait_ge(v_ready, (s + 2) * 2)
                pe.wait_ge(w_ready, (s + 1) * PAIRS + PAIRS - (QUADS - 1 - quad))
                if quad == 0 and norm:
                    pe.wait_ge(xt_lo, (s + 3) * DH)
                else:
                    pe.wait_ge(num_ready, (s + 1) * QUADS + quad)
                    pe.wait_ge(den_ready, (s + 1) * QUADS + quad)
                pairs = range(quad * PAIRS // QUADS, (quad + 1) * PAIRS // QUADS)
                for j, pair in enumerate(pairs):
                    pe.matmul(misc[0][PW * j:PW * (j + 1), :], v[:, 1 - par, PW * pair:PW * (pair + 1)],
                              w_exp[:, pair], start=True, stop=True)
                for j, pair in enumerate(pairs):
                    mm = pe.matmul(misc[1][PW * j:PW * (j + 1), :], head_ones[:], w_exp[:, pair],
                                   start=True, stop=True)
                mm.then_inc(pv_psum, 1)

            def step(s, par, ffn, attention, norm, load):
                first, second = tile_steps(s, ffn)
                if attention:
                    scores(s, 0)
                    scores(s, 1)
                for i in range(LAG, NH):
                    if i == 3 and norm and par == 0:
                        transpose_keys(s)
                    if i == 5 and norm and par == 0:
                        keys_values(s)
                    if i == 6 and norm and par == 0:
                        transpose_k(s)
                    if i == NH - 1 and norm:
                        transpose_x(s, par)
                    if i in first:
                        first_product(past(s), first[i], par if ffn else 1 - par)
                    if attention and i > LAG:
                        scores(s, i - 1)
                    if i in second:
                        second_product(past(s), second[i])
                if ffn:
                    second_product(s, NH - 2)
                if attention:
                    scores(s, NH - 1)
                if norm:
                    for m in range(DH):
                        queries(s, par, m)
                if ffn:
                    second_product(s, NH - 1)
                if attention:
                    weighted_values(s, 0, par, norm)
                segment, tail = tail_tiles(s, attention)
                for i in tail:
                    first_product(segment, i, 1 - par if attention else par, norm)
                if attention:
                    weighted_values(s, 1, par, norm)
                if ffn:
                    output_product(s, par)

            pe.wait_ge(consts_made, 3)
            pe.wait_ge(masks_made, 4)
            pe.transpose(s_bank[1][:, 0:P], k_mask_t[:], identity[:]).then_inc(k_mask_psum, 1)

            def first_step():
                transpose_keys(-2)
                transpose_x(-2, 0)
                keys_values(-2)
                queries(-2, 0, 0)
                transpose_k(-2)
                queries(-2, 0, 1)
                for i in range(LAG):
                    first_product(0, i, 0)

            iterations(pe, first_step, step)


def kernel(L0_attn_x, L0_attn_Wqkv, L0_attn_Wout, L0_ffn_W1, L0_ffn_b1, L0_ffn_W2, L0_ffn_b2):
    import numpy as np
    import concourse.bacc as bacc
    from concourse.bass_utils import run_bass_kernel_spmd

    wqkv = np.asarray(L0_attn_Wqkv)
    arrays = {
        "x": np.asarray(L0_attn_x),
        "wq_t": wqkv[:D].T,
        "wkv_t": wqkv[D:].T,
        "wout_t": np.asarray(L0_attn_Wout).T,
        "w1": np.asarray(L0_ffn_W1),
        "b1": np.asarray(L0_ffn_b1).reshape(-1, P).T,
        "w2": np.asarray(L0_ffn_W2),
        "b2": np.asarray(L0_ffn_b2),
    }
    arrays = {name: np.ascontiguousarray(a) for name, a in arrays.items()}
    nc = bacc.Bacc("TRN2", target_bir_lowering=False, num_devices=1)
    args = [nc.dram_tensor(name, a.shape, mybir.dt.from_np(a.dtype), kind="ExternalInput").ap()
            for name, a in arrays.items()]
    out = nc.dram_tensor("out", arrays["x"].shape, F32, kind="ExternalOutput").ap()
    ln_attention_ffn(nc, *args, out)
    r = run_bass_kernel_spmd(nc, [arrays], core_ids=[0])
    return r.results[0]["out"]
```
